# Optimizing a Trainium2 kernel written in Bass

```python
import numpy as np
import jax
import jax.numpy as jnp

def _softmax(x, axis=-1):
    return jax.nn.softmax(x, axis=axis)

def _gelu(x):
    return jax.nn.gelu(x, approximate=True)

def _silu(x):
    return jax.nn.silu(x)

def _sigmoid(x):
    return jax.nn.sigmoid(x)

def _layernorm(x, axis=-1, eps=1e-05):
    m = jnp.mean(x, axis=axis, keepdims=True)
    v = jnp.var(x, axis=axis, keepdims=True)
    return (x - m) / jnp.sqrt(v + eps)

def _scatter_add(tgt, idx, src, axis=0):
    return tgt.at[idx].add(src)

def _segment_sum(src, seg, n):
    return jax.ops.segment_sum(src, seg, n)
kernel_name = 'mk_adj_preln_d2_adj_r2_cf1ab8'

def setup_inputs(seed: int=0):
    np.random.seed(seed)
    _w = jnp.asarray

    def _rec_inputs():
        import jax
        import jax.numpy as jnp
        _gk = jax.random.key(seed)
        x = -0.000929 + 1 * jax.random.normal(jax.random.fold_in(_gk, 1), (4096, 128), jnp.float32)
        _a = jax.random.bernoulli(jax.random.fold_in(_gk, 2), 0.00195312, (4096, 4096))
        _a = jnp.logical_or(_a, jnp.swapaxes(_a, -1, -2))
        _a = jnp.logical_or(_a, jnp.eye(4096, dtype=bool))
        _af = _a.astype(jnp.float32)
        _af = _af * jax.random.uniform(jax.random.fold_in(_gk, 3), (4096, 4096), jnp.float32, 0.05, 1)
        adj = _af
        return (x, adj)
    x, adj = _rec_inputs()

    def _L0_gnn_setup():
        import jax, jax.numpy as jnp
        import numpy as np
        N = 4096
        F_IN = 128
        F_OUT = 128
        ALPHA = 0.2
        NEG_INF = -9000000000000000.0

        def _signed_adj(key, n, p=0.002):
            r = jax.random.uniform(key, (n, n), dtype=jnp.float32)
            return jnp.where(r < p, 1.0, jnp.where(r > 1.0 - p, -1.0, 0.0)).astype(jnp.float32)
        key = jax.random.key(seed)
        k_h, k_na, k_ea, k_w, k_a = jax.random.split(key, 5)
        h = jax.random.normal(k_h, (N, F_IN), dtype=jnp.float32)
        node_adj = _signed_adj(k_na, N)
        edge_adj = _signed_adj(k_ea, N)
        lim_w = 1.414 * np.sqrt(6.0 / (F_IN + F_OUT))
        W = jax.random.uniform(k_w, (F_IN, F_OUT), dtype=jnp.float32, minval=-lim_w, maxval=lim_w)
        lim_a = 1.414 * np.sqrt(6.0 / (2 * F_OUT + 1))
        a = jax.random.uniform(k_a, (2 * F_OUT, 1), dtype=jnp.float32, minval=-lim_a, maxval=lim_a)
        return {'h': h, 'node_adj': node_adj, 'edge_adj': edge_adj, 'W': W, 'a': a}
    _L0_gnn_all = _L0_gnn_setup()
    _L0_gnn_in = {k: v for k, v in _L0_gnn_all.items() if k in ('W', 'a')}
    del _L0_gnn_all

    def _L1_gnn_setup():
        import jax, jax.numpy as jnp
        import numpy as np
        NEG_SLOPE = 0.01
        N_U, N_V = (4096, 4096)
        U_F, V_F = (128, 128)
        HIDS = [128, 128]
        NUM_ROUNDS = 3

        def _glorot(key, fan_in, fan_out):
            lim = np.sqrt(6.0 / (fan_in + fan_out)).astype(np.float32)
            return jax.random.uniform(key, (fan_in, fan_out), jnp.float32, -lim, lim)

        def _mlp(x, W1, b1, W2, b2, W3, b3):
            a = jax.nn.leaky_relu
            x = a(x @ W1 + b1, NEG_SLOPE)
            x = a(x @ W2 + b2, NEG_SLOPE)
            return a(x @ W3 + b3, NEG_SLOPE)
        key = jax.random.key(seed)
        ks = jax.random.split(key, 12)
        inp = {'u_node_feats': jax.random.normal(ks[0], (N_U, U_F), jnp.float32), 'v_node_feats': jax.random.normal(ks[1], (N_V, V_F), jnp.float32), 'uv_adj_mat': jax.random.uniform(ks[2], (N_V, N_U), jnp.float32), 'vu_adj_mat': jax.random.uniform(ks[3], (N_U, N_V), jnp.float32)}
        dims_uv = [U_F] + HIDS + [V_F]
        dims_vu = [V_F] + HIDS + [U_F]
        k = 4
        for tag, dims in (('uv', dims_uv), ('vu', dims_vu)):
            for i in range(3):
                inp[f'{tag}_W{i + 1}'] = _glorot(ks[k], dims[i], dims[i + 1])
                k += 1
                inp[f'{tag}_b{i + 1}'] = jnp.zeros((dims[i + 1],), jnp.float32)
        return inp
    _L1_gnn_all = _L1_gnn_setup()
    _L1_gnn_in = {k: v for k, v in _L1_gnn_all.items() if k in ('v_node_feats', 'uv_W1', 'uv_b1', 'uv_W2', 'uv_b2', 'uv_W3', 'uv_b3', 'vu_W1', 'vu_b1', 'vu_W2', 'vu_b2', 'vu_W3', 'vu_b3')}
    del _L1_gnn_all
    return {'x': x, 'adj': adj, 'L0_gnn_W': _L0_gnn_in['W'], 'L0_gnn_a': _L0_gnn_in['a'], 'L1_gnn_v_node_feats': _L1_gnn_in['v_node_feats'], 'L1_gnn_uv_W1': _L1_gnn_in['uv_W1'], 'L1_gnn_uv_b1': _L1_gnn_in['uv_b1'], 'L1_gnn_uv_W2': _L1_gnn_in['uv_W2'], 'L1_gnn_uv_b2': _L1_gnn_in['uv_b2'], 'L1_gnn_uv_W3': _L1_gnn_in['uv_W3'], 'L1_gnn_uv_b3': _L1_gnn_in['uv_b3'], 'L1_gnn_vu_W1': _L1_gnn_in['vu_W1'], 'L1_gnn_vu_b1': _L1_gnn_in['vu_b1'], 'L1_gnn_vu_W2': _L1_gnn_in['vu_W2'], 'L1_gnn_vu_b2': _L1_gnn_in['vu_b2'], 'L1_gnn_vu_W3': _L1_gnn_in['vu_W3'], 'L1_gnn_vu_b3': _L1_gnn_in['vu_b3']}

def reference(x, adj, L0_gnn_W, L0_gnn_a, L1_gnn_v_node_feats, L1_gnn_uv_W1, L1_gnn_uv_b1, L1_gnn_uv_W2, L1_gnn_uv_b2, L1_gnn_uv_W3, L1_gnn_uv_b3, L1_gnn_vu_W1, L1_gnn_vu_b1, L1_gnn_vu_W2, L1_gnn_vu_b2, L1_gnn_vu_W3, L1_gnn_vu_b3):
    import jax
    import jax.numpy as jnp

    def _L0_gnn_ref(h, node_adj, edge_adj, W, a):
        import jax, jax.numpy as jnp
        import numpy as np
        N = 4096
        F_IN = 128
        F_OUT = 128
        ALPHA = 0.2
        NEG_INF = -9000000000000000.0

        def _signed_adj(key, n, p=0.002):
            r = jax.random.uniform(key, (n, n), dtype=jnp.float32)
            return jnp.where(r < p, 1.0, jnp.where(r > 1.0 - p, -1.0, 0.0)).astype(jnp.float32)
        hw = h @ W
        pos = (node_adj > 0).astype(hw.dtype)
        neg = (node_adj < 0).astype(hw.dtype)
        h_plus = pos @ hw
        h_minus = neg @ hw
        a1, a2 = (a[:F_OUT], a[F_OUT:])
        e_plus = jax.nn.leaky_relu((h_plus @ a1 + h_minus @ a2)[:, 0], ALPHA)
        e_minus = jax.nn.leaky_relu((h_minus @ a1 + h_plus @ a2)[:, 0], ALPHA)
        scores = jnp.where(edge_adj > 0, e_plus[None, :], NEG_INF)
        scores = jnp.where(edge_adj < 0, e_minus[None, :], scores)
        attn = jax.nn.softmax(scores, axis=1)
        h_prime = attn * edge_adj @ hw
        return h_prime

    def _L1_gnn_ref(u_node_feats, v_node_feats, uv_adj_mat, vu_adj_mat, uv_W1, uv_b1, uv_W2, uv_b2, uv_W3, uv_b3, vu_W1, vu_b1, vu_W2, vu_b2, vu_W3, vu_b3):
        import jax, jax.numpy as jnp
        import numpy as np
        NEG_SLOPE = 0.01
        N_U, N_V = (4096, 4096)
        U_F, V_F = (128, 128)
        HIDS = [128, 128]
        NUM_ROUNDS = 3

        def _glorot(key, fan_in, fan_out):
            lim = np.sqrt(6.0 / (fan_in + fan_out)).astype(np.float32)
            return jax.random.uniform(key, (fan_in, fan_out), jnp.float32, -lim, lim)

        def _mlp(x, W1, b1, W2, b2, W3, b3):
            a = jax.nn.leaky_relu
            x = a(x @ W1 + b1, NEG_SLOPE)
            x = a(x @ W2 + b2, NEG_SLOPE)
            return a(x @ W3 + b3, NEG_SLOPE)
        u, v = (u_node_feats, v_node_feats)
        for _ in range(NUM_ROUNDS):
            v = _mlp(uv_adj_mat @ u, uv_W1, uv_b1, uv_W2, uv_b2, uv_W3, uv_b3)
            u = _mlp(vu_adj_mat @ v, vu_W1, vu_b1, vu_W2, vu_b2, vu_W3, vu_b3)
        return v
    h = jnp.maximum(_layernorm(x, axis=-1), 0.0)
    x = x + _L0_gnn_ref(h, adj, adj, L0_gnn_W, L0_gnn_a)
    h = jnp.maximum(_layernorm(x, axis=-1), 0.0)
    x = x + _L1_gnn_ref(h, L1_gnn_v_node_feats, adj, adj, L1_gnn_uv_W1, L1_gnn_uv_b1, L1_gnn_uv_W2, L1_gnn_uv_b2, L1_gnn_uv_W3, L1_gnn_uv_b3, L1_gnn_vu_W1, L1_gnn_vu_b1, L1_gnn_vu_W2, L1_gnn_vu_b2, L1_gnn_vu_W3, L1_gnn_vu_b3)
    return x

_drawn_inputs = setup_inputs


def setup_inputs(seed=0):
    import zlib

    import numpy as np

    out = dict(_drawn_inputs(seed))
    spreads = {'L1_gnn_uv_b1': (0.0, 0.563),
     'L1_gnn_uv_b2': (0.0, 0.527),
     'L1_gnn_uv_b3': (0.0, 0.307),
     'L1_gnn_vu_b1': (0.0, 0.8),
     'L1_gnn_vu_b2': (0.0, 0.799),
     'L1_gnn_vu_b3': (0.0, 0.602)}
    factors = {'x': 3.353, 'L0_gnn_a': 5.139}
    for name, (base, spread) in spreads.items():
        noise = np.random.default_rng([zlib.crc32(name.encode()), seed]).standard_normal(out[name].shape)
        drawn = base * np.exp(spread * noise) if base else spread * noise
        out[name] = jnp.asarray(drawn.astype(out[name].dtype))
    for name, factor in factors.items():
        out[name] = (out[name] * factor).astype(out[name].dtype)
    return out
```

```python
from contextlib import ExitStack

import concourse.bass as bass
from concourse import mybir

P = 128
N = 4096
BLOCKS = N // P
COLS = 512
CHUNKS = N // COLS
PER = COLS // P
UB = 2
UNITS = BLOCKS // UB
UW = UB * COLS
KEPT = 2
RING = 7
STREAMED = UNITS - KEPT
LAPS = STREAMED // RING
SPLIT = 4
ROUNDS = 5
EPS = 1e-5
SLOPE = 0.01
E_SLOPE = 0.2
TOP = 75.0
LEAST = 1e-30
HUGE = 3.0e38
TINY = 1e-37

F32 = mybir.dt.float32
F32R = mybir.dt.float32r
BF16 = mybir.dt.bfloat16
I32 = mybir.dt.int32
ALU = mybir.AluOpType
ACT = mybir.ActivationFunctionType
AX = mybir.AxisListType
RMAX = bass.bass_isa.ReduceOp.max

W0, UV, VU, B3UV, B3VU, IDENT, A12, BIAS = 0, 128, 512, 896, 1024, 1152, 1280, 1282
PARAMS = 1286
G_LINKS = 2 + BLOCKS * (5 + 3)
LN_LINKS = 7
MERGE_LINKS = 3


def build(nc, x_in, adj, params_in, out, hw_dram):
    assert STREAMED % RING == 0 and UNITS % SPLIT == 0
    ctx = ExitStack()
    with ctx:
        def sb(name, shape, dt):
            return ctx.enter_context(nc.sbuf_tensor(name, shape, dt))

        def sem(name):
            return ctx.enter_context(nc.semaphore(name))

        params = sb("params", [P, PARAMS], F32)
        x_sb = sb("x_sb", [P, N], F32)
        stage = sb("stage", [P, N], F32)
        u_hi = sb("u_hi", [P, N], F32R)
        scratch_at = nc.sbuf_base
        u_lo = sb("u_lo", [P, N], F32R)
        scratch = nc.alloc_sbuf_tensor_at("scratch", [P, N], F32, offset=scratch_at)
        kept = sb("kept", [P, CHUNKS, KEPT * UW], F32)
        ring = sb("ring", [P, RING, UW], F32)
        a_hi = sb("a_hi", [P, SPLIT, UW], F32R)
        a_lo = sb("a_lo", [P, SPLIT, UW], F32R)
        pos = sb("pos", [P, 2, UW], BF16)
        y = sb("y", [P, COLS], F32)
        h1 = sb("h1", [P, COLS], F32)
        h2 = sb("h2", [P, COLS], F32)
        probe = sb("probe", [P, BLOCKS, 14], BF16)
        wpart = sb("wpart", [P, BLOCKS, 3], BF16)
        p_all = sb("p_all", [P, BLOCKS, 2], F32)
        rest = sb("rest", [P, BLOCKS, 2], F32)
        e_all = sb("e_all", [P, BLOCKS, 7], F32)
        e_sum = sb("e_sum", [P, BLOCKS, 2], F32)
        e_pm = sb("e_pm", [P, BLOCKS, 2], F32)
        w_all = sb("w_all", [P, BLOCKS], F32)
        den_all = sb("den_all", [P, BLOCKS], F32)
        var_all = sb("var_all", [P, BLOCKS], F32)
        bad = sb("bad", [P, 4], F32)
        flag = sb("flag", [P, 1], I32)
        top = sb("top", [P, 2], F32)
        stats = sb("stats", [P, PER, 6], F32)
        mv = sb("mv", [P, PER, 2], F32)
        small = sb("small", [P, 8, PER], F32)
        ones = sb("ones", [P, P], F32)
        gate = sb("gate", [P, 2], F32)
        pick = sb("pick", [P, 3], F32)
        psum = ctx.enter_context(nc.psum_tensor("psum", [P, 8, COLS], F32))
        acc = [psum[:, 0, :], psum[:, 1, :]]
        row = [psum[:, 2, :], psum[:, 3, :]]
        z1, z2, tp, tiny = (psum[:, k, :] for k in (4, 5, 6, 7))

        ident = params[:, IDENT:IDENT + P]
        a12 = params[:, A12:A12 + 2]
        masks = scratch[:, :].bitcast(BF16).rearrange("p (s g c) -> p s g c", s=SPLIT, g=2)
        fb = scratch[:, :].rearrange("p (k c) -> p k c", c=COLS)
        g_a = [fb[:, 0, :], fb[:, 1, :]]
        g_row, g_neg, g_t, g_e, g_num, g_den = (fb[:, k, :] for k in range(2, 8))
        g_s = h1[:, :]
        g_hw = [h2[:, 0:P], h2[:, P:2 * P]]
        e_plus, e_minus = e_pm[:, :, 0], e_pm[:, :, 1]

        class Mlp:
            def __init__(self, at, b3, b):
                self.w = [params[:, at + k * P:at + (k + 1) * P] for k in range(3)]
                self.b1, self.b2 = params[:, BIAS + b:BIAS + b + 1], params[:, BIAS + b + 1:BIAS + b + 2]
                self.b3 = params[:, b3:b3 + P].unsqueeze(1).broadcast_to([P, PER, P])

        uv, vu = Mlp(UV, B3UV, 0), Mlp(VU, B3VU, 2)

        params_in_sb, x_in_sb, kept_in = sem("params_in_sb"), sem("x_in_sb"), sem("kept_in")
        landed = [sem(f"landed{s}") for s in range(RING)]
        hw_out, hw_done, out_done = sem("hw_out"), sem("hw_done"), sem("out_done")
        ones_set = sem("ones_set")

        def norm_sems(tag):
            return {k: sem(f"{tag}_{k}") for k in ("chain", "var", "std", "done")}

        first = norm_sems("first")
        pre_t, pre_y, pre_hwt, pre_h1, pre_hw, pre_st, pre_p, pre_pc = (
            sem(f"pre_{k}") for k in ("turned", "y", "hwt", "h1", "hw", "stage", "p", "pcopied"))
        masked, mask_used = sem("masked"), sem("mask_used")
        e_row, e_turned, e_col = sem("e_row"), sem("e_turned"), sem("e_col")
        chain = sem("chain")
        probe_set, top_part, top_all, shifted, w_exp, w_set = (
            sem(k) for k in ("probe_set", "top_part", "top_all", "shifted", "w_exp", "w_set"))
        u_hi_set, u_lo_set = sem("u_hi_set"), sem("u_lo_set")
        hi_set, lo_set, unit_used, pos_set = sem("hi_set"), sem("lo_set"), sem("unit_used"), sem("pos_set")
        bias1_set, bias2_set = sem("bias1_set"), sem("bias2_set")
        y_set, z1_set, h1_set, z2_set, h2_set, z3_set, t3_set, fresh = (
            sem(k) for k in ("y_set", "z1_set", "h1_set", "z2_set", "h2_set", "z3_set", "t3_set", "fresh"))

        def merge_sems(tag):
            got = norm_sems(tag)
            got.update({k: sem(f"{tag}_{k}") for k in ("copied", "turned")})
            return got

        fast, slow = merge_sems("fast"), merge_sems("slow")
        bad_set, bad_sum, flag_set = sem("bad_set"), sem("bad_sum"), sem("flag_set")
        final = sem("final")
        g_landed = [sem("g_landed0"), sem("g_landed1")]
        hw_landed = [sem("hw_landed0"), sem("hw_landed1")]
        g_x, g_freed, g_chain, g_all, g_arg, g_exp, g_tile, g_prod = (
            sem(f"g_{k}") for k in ("x", "freed", "chain", "all", "arg", "exp", "tile", "prod"))

        block = ctx.enter_context(nc.Block())

        def wait(eng, s, value):
            if not isinstance(value, int) or value > 0:
                eng.wait_ge(s, value)

        class Link:

            def __init__(self, s, base=0):
                self.s, self.base, self.k = s, base, 0

            def __call__(self, ins, gated=False):
                self.k += 1
                ins.then_inc(self.s, 1)
                nc.vector.wait_ge(self.s, self.base + self.k)
                if gated:
                    nc.vector.memset(gate[:, 0:1], 0.0)

        def chunk_cols(c):
            return bass.ds(c * COLS, COLS) if not isinstance(c, int) else slice(c * COLS, (c + 1) * COLS)

        def unit_raw(c, u):
            return kept[:, c, u * UW:(u + 1) * UW] if u < KEPT else ring[:, (u - KEPT) % RING, :]

        def wait_raw(eng, t, u):
            if u >= KEPT:
                n = u - KEPT
                eng.wait_ge(landed[n % RING], 16 * (LAPS * t + n // RING + 1))

        A_PASS, M_PASS = CHUNKS, 2 * CHUNKS

        @block.sync
        def _(sp):
            def load(c, u, n):
                sp.dma_start(ring[:, n % RING, :], adj[c * UNITS + u]).then_inc(landed[n % RING], 16)

            sp.dma_start(params[:, :], params_in).then_inc(params_in_sb, 16)
            for q in range(4):
                sp.dma_start(x_sb[:, q * 1024:(q + 1) * 1024],
                             x_in[:, q * 1024:(q + 1) * 1024]).then_inc(x_in_sb, 16)
            for c in range(CHUNKS):
                for k in range(KEPT):
                    sp.dma_start(kept[:, c, k * UW:(k + 1) * UW], adj[c * UNITS + k]).then_inc(kept_in, 16)

            def first_pass(c):
                for n in range(STREAMED):
                    wait(sp, masked, c * UNITS + n + KEPT - RING + 1 if n >= RING
                         else (c - 1) * UNITS + n + KEPT + RING + 1)
                    load(c, n + KEPT, n)

            def later(c, t, since, n):
                v = (t - A_PASS) * UNITS + n + KEPT - RING + 1 if n >= RING \
                    else (t - A_PASS - 1) * UNITS + n + KEPT + RING + 1
                if since == 0 and n < RING:
                    sp.wait_ge(masked, CHUNKS * UNITS)
                else:
                    sp.wait_ge(hi_set, v)
                    sp.wait_ge(lo_set, v)
                load(c, n + KEPT, n)

            first_pass(0)
            with sp.Fori(1, CHUNKS) as c:
                first_pass(c)
            for n in range(STREAMED):
                later(0, A_PASS, 0, n)
            with sp.Fori(1, CHUNKS) as c:
                for n in range(STREAMED):
                    later(c, A_PASS + c, 1, n)
            for n in range(RING):
                later(0, M_PASS, 1, n)

            sp.wait_ge(flag_set, 1)
            sp.wait_ge(hw_done, 16)
            with sp.If(sp.value_load(flag[0:1, 0:1], min_val=0, max_val=P) != 0):
                sp.dma_start(stage[:, :], x_in).then_inc(g_x, 16)
                with sp.Fori(0, CHUNKS) as c:
                    for phase in range(2):
                        with sp.Fori(0, UNITS) as u:
                            for b in range(UB):
                                m = (c * 2 + phase) * BLOCKS + u * UB
                                sp.wait_ge(g_freed, m)
                                if phase:
                                    sp.wait_ge(g_prod, c * BLOCKS + u * UB)
                                    sp.dma_start(g_hw[b], hw_dram[:, bass.ds(u * (UB * P) + b * P, P)]) \
                                        .then_inc(hw_landed[b], 16)
                                sp.dma_start(g_a[b], adj[c * UNITS + u][:, b * COLS:(b + 1) * COLS]) \
                                    .then_inc(g_landed[b], 16)

            for n in range(RING, STREAMED):
                later(0, M_PASS, 1, n)
            with sp.Fori(1, CHUNKS) as c:
                for n in range(STREAMED):
                    later(c, M_PASS + c, 1, n)
            with sp.Fori(1, ROUNDS) as r:
                with sp.Fori(0, CHUNKS) as c:
                    for n in range(STREAMED):
                        later(c, M_PASS + r * CHUNKS + c, 1, n)
            for c in range(CHUNKS):
                sp.wait_ge(final, c + 1)
                sp.dma_start(out[:, c * COLS:(c + 1) * COLS], stage[:, c * COLS:(c + 1) * COLS]) \
                    .then_inc(out_done, 16)
            sp.wait_ge(out_done, 16 * CHUNKS)

        @block.gpsimd
        def _(pool):
            nc.gpsimd.memset(ones[:, :], 1.0)
            nc.gpsimd.memset(pick[:, 0:1], 1.0)
            nc.gpsimd.memset(pick[:, 1:3], 0.0).then_inc(ones_set, 1)
            pool.wait_ge(top_part, 1)
            nc.gpsimd.partition_all_reduce(top[:, 1:2], top[:, 0:1], P, RMAX).then_inc(top_all, 1)
            pool.wait_ge(flag_set, 1)
            with pool.If(pool.value_load(flag[0:1, 0:1], min_val=0, max_val=P) != 0):
                with pool.Fori(0, CHUNKS) as c:
                    pool.wait_ge(g_freed, (2 * c + 1) * BLOCKS)
                    nc.gpsimd.tensor_tensor(gate[:, 1:2], pick[:, 0:1], pick[:, 1:2], ALU.mult)
                    nc.gpsimd.partition_all_reduce(g_e, g_row, P, RMAX).then_inc(g_all, 1)

        @block.scalar
        def _(act):
            with act.Fori(0, CHUNKS) as c:
                act.wait_ge(first["var"], c + 1)
                act.activation(small[:, 1, :], small[:, 0, :], ACT.Sqrt).then_inc(first["std"], 1)
                act.wait_ge(pre_t, c + 1)
                act.wait_ge(pre_hw, c)
                act.activation(y[:, :], tp, ACT.Copy).then_inc(pre_y, 1)
                act.wait_ge(pre_hwt, c + 1)
                act.wait_ge(pre_p, c)
                act.activation(h1[:, :], z1, ACT.Copy).then_inc(pre_h1, 1)
            act.wait_ge(pre_st, CHUNKS)
            act.dma_start(hw_dram, stage[:, :]).then_inc(hw_done, 16)

            def e_copy(c, par):
                act.wait_ge(mask_used, (c + 1) * UNITS)
                wait(act, e_turned, c)
                act.activation(y[0:7, :], row[par][0:7, :], ACT.Copy).then_inc(e_row, 1)

            with act.Fori(0, CHUNKS // 2) as k:
                for par in range(2):
                    e_copy(2 * k + par, par)

            act.wait_ge(shifted, 1)
            act.activation(w_all[:, :], e_sum[:, :, 0], ACT.Exp).then_inc(w_exp, 1)
            act.wait_ge(w_exp, 1)
            for b in range(BLOCKS):
                act.activation(u_hi[:, b * P:(b + 1) * P], stage[:, b * P:(b + 1) * P], ACT.Copy,
                               scale=w_all[:, b:b + 1]).then_inc(u_hi_set, 1)

            def split_hi(c, t, u):
                v = (t - A_PASS) * UNITS + u
                wait_raw(act, t, u)
                wait(act, unit_used, v - SPLIT + 1)
                act.activation(a_hi[:, u % SPLIT, :], unit_raw(c, u), ACT.Copy).then_inc(hi_set, 1)

            def merge_copy(n, s, num, den):
                if s is fast:
                    act.wait_ge(unit_used, (n + 1) * UNITS)
                else:
                    act.wait_ge(g_prod, (n + 1) * BLOCKS)
                wait(act, s["turned"], n)
                act.activation(y[:, :], num, ACT.Copy)
                act.activation(h2[0:3, :], den[0:3, :], ACT.Copy).then_inc(s["copied"], 1)

            def merge_root(n, s):
                act.wait_ge(s["var"], n + 1)
                act.activation(small[:, 1, :], small[:, 0, :], ACT.Sqrt).then_inc(s["std"], 1)

            def attention(c, par, prev):
                for u in range(UNITS):
                    split_hi(c, A_PASS + c, u)
                    if prev and u == 3:
                        merge_copy(c - 1, fast, acc[1 - par], row[1 - par])
                    if prev and u == 9:
                        merge_root(c - 1, fast)

            act.wait_ge(kept_in, 16 * CHUNKS * KEPT)
            attention(0, 0, False)
            attention(1, 1, True)
            with act.Fori(1, CHUNKS // 2) as k:
                for par in range(2):
                    attention(2 * k + par, par, True)
            merge_copy(CHUNKS - 1, fast, acc[1], row[1])
            merge_root(CHUNKS - 1, fast)

            act.wait_ge(flag_set, 1)
            with act.If(act.value_load(flag[0:1, 0:1], min_val=0, max_val=P) != 0):
                with act.Fori(0, CHUNKS) as c:
                    with act.Fori(0, BLOCKS) as j:
                        for s in range(2):
                            act.wait_ge(g_arg, c * (2 * BLOCKS) + j * 2 + s + 1)
                            act.activation(g_e, g_t, ACT.Exp).then_inc(g_exp, 1)
                    merge_copy(c, slow, acc[0], row[0])
                    merge_root(c, slow)
                act.wait_ge(slow["done"], CHUNKS)

            def y_copy(m, par):
                act.wait_ge(unit_used, (CHUNKS + m + 1) * UNITS)
                wait(act, z1_set, m)
                act.activation(y[:, :], acc[par], ACT.Copy).then_inc(y_set, 1)

            def bias1(m, mlp):
                act.wait_ge(z1_set, m + 1)
                wait(act, fresh, m)
                act.activation(h1[:, :], z1, ACT.Identity, bias=mlp.b1).then_inc(bias1_set, 1)

            def bias2(m, mlp):
                act.wait_ge(z2_set, m + 1)
                wait(act, z3_set, m)
                act.activation(h2[:, :], z2, ACT.Identity, bias=mlp.b2).then_inc(bias2_set, 1)

            def fill_hi(m, s):
                act.activation(u_hi[:, s * COLS:(s + 1) * COLS], stage[:, s * COLS:(s + 1) * COLS],
                               ACT.Copy).then_inc(u_hi_set, 1)

            def passing(m, c, par, mlp, prev, start):
                for u in range(UNITS):
                    split_hi(c, M_PASS + m, u)
                    if prev and u == 2:
                        y_copy(m - 1, 1 - par)
                    if start and u == 2:
                        act.wait_ge(unit_used, (CHUNKS + m) * UNITS)
                        wait(act, fresh, m - 1)
                        fill_hi(m, 0)
                        fill_hi(m, 1)
                    if start and 3 <= u <= 7:
                        fill_hi(m, u - 1)
                    if prev and u == 5:
                        bias1(m - 1, mlp)
                    if prev and u == 8:
                        bias2(m - 1, mlp)
                    if start and u == 13:
                        wait(act, fresh, m)
                        fill_hi(m, 7)

            def a_round(r, mlp, prev_mlp):
                m = r * CHUNKS
                passing(m, 0, 0, prev_mlp, prev_mlp is not None, True)
                passing(m + 1, 1, 1, mlp, True, False)
                with act.Fori(1, CHUNKS // 2) as k:
                    for par in range(2):
                        passing(m + 2 * k + par, 2 * k + par, par, mlp, True, False)

            act.wait_ge(fast["done"], CHUNKS)
            a_round(0, uv, None)
            with act.Fori(0, (ROUNDS - 1) // 2) as q:
                a_round(2 * q + 1, vu, uv)
                a_round(2 * q + 2, uv, vu)
            m = ROUNDS * CHUNKS - 1
            y_copy(m, 1)
            bias1(m, uv)
            bias2(m, uv)

        @block.vector
        def _(dve):
            def layer_norm(n, s, links, source, target, whole):
                for b in range(PER):
                    ins = dve.bn_stats(stats[:, b, :], source(b))
                links(ins, True)
                for b in range(PER):
                    ins = dve.bn_aggr(mv[:, b, :], stats[:, b, :])
                links(ins)
                dve.tensor_scalar(small[:, 0, :], mv[:, :, 1], EPS, None, ALU.add).then_inc(s["var"], 1)
                dve.wait_ge(s["std"], n + 1)
                links(dve.reciprocal(small[:, 2, :], small[:, 1, :]))
                links(dve.tensor_tensor(small[:, 3, :], small[:, 2, :], small[:, 2, :], ALU.mult))
                dve.wait_ge(s["var"], n + 1)
                links(dve.tensor_tensor(small[:, 4, :], small[:, 3, :], small[:, 0, :], ALU.mult))
                links(dve.tensor_scalar(small[:, 5, :], small[:, 4, :], -0.5, 1.5, ALU.mult, ALU.add))
                links(dve.tensor_tensor(small[:, 6, :], small[:, 5, :], small[:, 2, :], ALU.mult))
                for b in range(PER):
                    ins = dve.tensor_scalar(target(b), source(b), mv[:, b, 0:1], small[:, 6, b:b + 1],
                                            ALU.subtract, ALU.mult)
                return ins

            dve.wait_ge(x_in_sb, 16 * 4)
            with dve.Fori(0, CHUNKS) as c:
                link = Link(first["chain"], c * (LN_LINKS + 1))
                dve.wait_ge(pre_t, c)
                dve.memset(gate[:, 0:1], 0.0)
                ins = layer_norm(c, first, link,
                                 lambda b: x_sb[:, bass.ds(c * COLS + b * P, P)],
                                 lambda b: h2[:, b * P:(b + 1) * P], None)
                link(ins)
                assert link.k == LN_LINKS + 1
                dve.tensor_scalar(h2[:, :], h2[:, :], 0.0, None, ALU.max).then_inc(first["done"], 1)
                dve.wait_ge(pre_hw, c + 1)
                dve.tensor_copy(stage[:, chunk_cols(c)], z2).then_inc(pre_st, 1)
                dve.wait_ge(pre_p, c + 1)
                dve.tensor_copy(p_all[:, bass.ds(c * PER, PER), :],
                                tiny[:, 0:2 * PER].rearrange("p (b k) -> p b k", k=2)).then_inc(pre_pc, 1)

            dve.wait_ge(pre_pc, CHUNKS)
            link = Link(chain)
            link(dve.memset(probe[:, :, :], 0.0))
            dve.memset(probe[:, :, 13], 1.0)
            source = p_all
            for part in range(3):
                for k in range(2):
                    ins = dve.tensor_copy(probe[:, :, 3 * k + part], source[:, :, k])
                link(ins)
                for k in range(2):
                    ins = dve.tensor_copy(probe[:, :, 10 - 3 * k + part], source[:, :, k])
                    if part < 2:
                        ins = dve.tensor_tensor(rest[:, :, k], source[:, :, k], probe[:, :, 3 * k + part],
                                                ALU.subtract)
                if part < 2:
                    link(ins)
                source = rest
            ins.then_inc(probe_set, 1)

            def e_cols(c):
                dve.wait_ge(e_turned, c + 1)
                cols = bass.ds(c * PER, PER) if not isinstance(c, int) else slice(c * PER, (c + 1) * PER)
                dve.tensor_copy(e_all[:, cols, :],
                                tiny[:, 0:8 * PER].rearrange("p (b k) -> p b k", k=8)[:, :, 0:7]) \
                    .then_inc(e_col, 1)

            def mask_chunk(c, prev):
                for u in range(UNITS):
                    wait_raw(dve, c, u)
                    wait(dve, mask_used, c * UNITS + u - SPLIT + 1)
                    dve.tensor_scalar(masks[:, u % SPLIT, 0, :], unit_raw(c, u), 0.0, None, ALU.is_gt)
                    dve.tensor_scalar(masks[:, u % SPLIT, 1, :], unit_raw(c, u), 0.0, None, ALU.is_lt) \
                        .then_inc(masked, 1)
                    if prev and u == 6:
                        e_cols(c - 1)

            dve.wait_ge(kept_in, 16 * CHUNKS * KEPT)
            mask_chunk(0, False)
            with dve.Fori(1, CHUNKS) as c:
                mask_chunk(c, True)
            e_cols(CHUNKS - 1)

            dve.wait_ge(e_col, CHUNKS)
            for k in range(2):
                ins = dve.tensor_reduce(e_sum[:, :, k], e_all[:, :, 3 * k:3 * k + 3], AX.X, ALU.add)
            link(ins)
            link(dve.scalar_tensor_tensor(out=e_pm[:, :, :], in0=e_sum[:, :, :], scalar=E_SLOPE, in1=e_sum[:, :, :],
                                          op0=ALU.mult, op1=ALU.max))
            dve.tensor_reduce(top[:, 0:1], e_plus, AX.X, ALU.max).then_inc(top_part, 1)
            dve.wait_ge(top_all, 1)
            dve.tensor_scalar(e_sum[:, :, 0], e_plus, top[:, 1:2], TOP, ALU.subtract, ALU.add) \
                .then_inc(shifted, 1)
            dve.wait_ge(w_exp, 1)
            source = w_all
            for part in range(3):
                ins = dve.tensor_copy(wpart[:, :, part], source[:, :])
                if part < 2:
                    link(ins)
                    link(dve.tensor_tensor(rest[:, :, 0], source[:, :], wpart[:, :, part], ALU.subtract))
                    source = rest[:, :, 0]
            ins.then_inc(w_set, 1)
            dve.wait_ge(mask_used, CHUNKS * UNITS)
            for b in range(BLOCKS):
                cols = slice(b * P, (b + 1) * P)
                dve.wait_ge(u_hi_set, b + 1)
                dve.scalar_tensor_tensor(out=u_lo[:, cols], in0=stage[:, cols], scalar=w_all[:, b:b + 1],
                                         in1=u_hi[:, cols].bitcast(F32), op0=ALU.mult, op1=ALU.subtract) \
                    .then_inc(u_lo_set, 1)

            def split_lo(c, t, u):
                dve.wait_ge(hi_set, (t - A_PASS) * UNITS + u + 1)
                dve.tensor_tensor(a_lo[:, u % SPLIT, :], unit_raw(c, u), a_hi[:, u % SPLIT, :].bitcast(F32),
                                  ALU.subtract).then_inc(lo_set, 1)

            def merge(n, s):
                def blk(t, b):
                    at = n * COLS + b * P
                    return t[:, at:at + P] if isinstance(n, int) else t[:, bass.ds(at, P)]

                def four(t):
                    return t[:, n * PER:(n + 1) * PER] if isinstance(n, int) else t[:, bass.ds(n * PER, PER)]

                link = Link(s["chain"], n * (LN_LINKS + MERGE_LINKS + 2))
                dve.wait_ge(s["turned"], n + 1)
                link(dve.tensor_reduce(four(den_all), tiny[:, 0:4 * PER].rearrange("p (b k) -> p b k", k=4)[:, :, 0:3],
                                       AX.X, ALU.add))
                link(dve.tensor_scalar(small[:, 7, :], four(den_all), TINY, None, ALU.max))
                link(dve.reciprocal(small[:, 7, :], small[:, 7, :]))
                for b in range(PER):
                    old = blk(x_sb, b) if s is fast else blk(stage, b)
                    ins = dve.scalar_tensor_tensor(out=blk(x_sb, b), in0=tp[:, b * P:(b + 1) * P],
                                                   scalar=small[:, 7, b:b + 1], in1=old,
                                                   op0=ALU.mult, op1=ALU.add)
                link(ins, True)
                ins = layer_norm(n, s, link, lambda b: blk(x_sb, b), lambda b: blk(stage, b), None)
                link(ins)
                assert link.k == LN_LINKS + MERGE_LINKS + 2, link.k
                dve.tensor_scalar(stage[:, chunk_cols(n)], stage[:, chunk_cols(n)], 0.0, None, ALU.max)
                dve.tensor_copy(four(var_all), small[:, 0, :]).then_inc(s["done"], 1)

            def attention(c, prev):
                for u in range(UNITS):
                    v = c * UNITS + u
                    wait_raw(dve, A_PASS + c, u)
                    wait(dve, unit_used, v - 1)
                    dve.tensor_scalar(pos[:, u % 2, :], unit_raw(c, u), 0.0, None, ALU.is_gt).then_inc(pos_set, 1)
                    split_lo(c, A_PASS + c, u)
                    if prev and u == 7:
                        merge(c - 1, fast)

            attention(0, False)
            dve.wait_ge(hw_done, 16)
            with dve.Fori(1, CHUNKS) as c:
                attention(c, True)
            merge(CHUNKS - 1, fast)

            dve.wait_ge(fast["done"], CHUNKS)
            dve.tensor_scalar(w_all[:, :], den_all[:, :], LEAST, None, ALU.is_ge)
            dve.tensor_scalar(rest[:, :, 0], var_all[:, :], HUGE, None, ALU.is_le)
            link(dve.tensor_scalar(rest[:, :, 1], e_all[:, :, 6], 0.5, None, ALU.is_lt))
            link(dve.tensor_tensor(w_all[:, :], w_all[:, :], rest[:, :, 0], ALU.mult))
            link(dve.tensor_tensor(w_all[:, :], w_all[:, :], rest[:, :, 1], ALU.mult))
            link(dve.tensor_reduce(bad[:, 0:1], w_all[:, :], AX.X, ALU.min))
            dve.tensor_scalar(bad[:, 1:2], bad[:, 0:1], -1.0, 1.0, ALU.mult, ALU.add).then_inc(bad_set, 1)
            dve.wait_ge(bad_sum, 1)
            dve.tensor_copy(flag[:, :], tiny[:, 0:1]).then_inc(flag_set, 1)

            dve.wait_ge(flag_set, 1)
            with dve.If(dve.value_load(flag[0:1, 0:1], min_val=0, max_val=P) != 0):
                def maxima(c, u, b):
                    m = 2 * c * BLOCKS + u * UB + b
                    j = u * UB + b
                    glink = Link(g_chain, c * G_LINKS + 1 + (u * UB + b) * 5)
                    a = g_a[b]
                    dve.wait_ge(g_landed[b], c * (2 * UNITS * 16) + u * 16 + 16)
                    for k, there, absent in ((0, ALU.is_gt, ALU.is_le), (1, ALU.is_lt, ALU.is_ge)):
                        dve.tensor_scalar(g_t, a, 0.0, e_pm[:, bass.ds(j, 1), k], there, ALU.mult)
                        glink(dve.tensor_scalar(g_s, a, 0.0, -HUGE, absent, ALU.mult))
                        glink(dve.tensor_tensor(g_t, g_t, g_s, ALU.add))
                        ins = dve.tensor_tensor(g_row, g_row, g_t, ALU.max)
                        if k == 0:
                            glink(ins)
                    ins.then_inc(g_freed, 1)
                    dve.wait_ge(g_freed, m + 1)

                def weights(c, u, b):
                    m = (2 * c + 1) * BLOCKS + u * UB + b
                    n = c * BLOCKS + u * UB + b
                    j = u * UB + b
                    glink = Link(g_chain, c * G_LINKS + 2 + BLOCKS * 5 + (u * UB + b) * 3)
                    a = g_a[b]
                    dve.wait_ge(g_landed[b], c * (2 * UNITS * 16) + (UNITS + 1) * 16 + u * 16)
                    dve.tensor_scalar(g_t, g_neg, e_pm[:, bass.ds(j, 1), 0], 0.0, ALU.add, ALU.min).then_inc(g_arg, 1)
                    dve.wait_ge(g_prod, n)
                    dve.wait_ge(g_exp, 2 * n + 1)
                    dve.scalar_tensor_tensor(out=g_num, in0=a, scalar=0.0, in1=g_e, op0=ALU.max, op1=ALU.mult)
                    glink(dve.scalar_tensor_tensor(out=g_den, in0=a, scalar=0.0, in1=g_e,
                                                   op0=ALU.is_gt, op1=ALU.mult))
                    dve.tensor_scalar(g_t, g_neg, e_pm[:, bass.ds(j, 1), 1], 0.0, ALU.add, ALU.min).then_inc(g_arg, 1)
                    dve.wait_ge(g_exp, 2 * n + 2)
                    glink(dve.scalar_tensor_tensor(out=g_s, in0=a, scalar=0.0, in1=g_e, op0=ALU.min, op1=ALU.mult))
                    glink(dve.tensor_tensor(g_num, g_num, g_s, ALU.add))
                    dve.scalar_tensor_tensor(out=g_s, in0=a, scalar=0.0, in1=g_e,
                                             op0=ALU.is_lt, op1=ALU.mult).then_inc(g_freed, 1)
                    dve.wait_ge(g_freed, m + 1)
                    dve.tensor_tensor(g_den, g_den, g_s, ALU.add).then_inc(g_tile, 1)

                dve.wait_ge(g_x, 16)
                with dve.Fori(0, CHUNKS) as c:
                    glink = Link(g_chain, c * G_LINKS)
                    glink(dve.memset(g_row, -HUGE), True)
                    with dve.Fori(0, UNITS) as u:
                        for b in range(UB):
                            maxima(c, u, b)
                    dve.wait_ge(g_all, c + 1)
                    dve.tensor_scalar(g_neg, g_e, -1.0, None, ALU.mult).then_inc(g_chain, 1)
                    dve.wait_ge(g_chain, c * G_LINKS + 2 + BLOCKS * 5)
                    dve.memset(gate[:, 0:1], 0.0)
                    with dve.Fori(0, UNITS) as u:
                        for b in range(UB):
                            weights(c, u, b)
                    merge(c, slow)
                    dve.wait_ge(slow["done"], c + 1)

            def fill_lo(n):
                s = n
                cols = slice(s * COLS, (s + 1) * COLS)
                dve.tensor_tensor(u_lo[:, cols], stage[:, cols], u_hi[:, cols].bitcast(F32), ALU.subtract) \
                    .then_inc(u_lo_set, 1)

            def leaky(h, ready, m, done):
                dve.wait_ge(ready, m + 1)
                dve.scalar_tensor_tensor(out=h[:, :], in0=h[:, :], scalar=SLOPE, in1=h[:, :],
                                         op0=ALU.mult, op1=ALU.max).then_inc(done, 1)

            def features(m, c, mlp):
                dve.wait_ge(z3_set, m + 1)
                dve.tensor_tensor(h1[:, :].rearrange("p (b f) -> p b f", b=PER),
                                  tp.rearrange("p (b f) -> p b f", b=PER), mlp.b3, ALU.add).then_inc(t3_set, 1)
                dve.wait_ge(t3_set, m + 1)
                dve.scalar_tensor_tensor(out=stage[:, chunk_cols(c)], in0=h1[:, :], scalar=SLOPE, in1=h1[:, :],
                                         op0=ALU.mult, op1=ALU.max).then_inc(fresh, 1)

            def passing(m, c, mlp, prev, start, r, prev_c):
                def fill(s):
                    dve.wait_ge(u_hi_set, BLOCKS + r * CHUNKS + s + 1)
                    fill_lo(s)

                for u in range(UNITS):
                    split_lo(c, M_PASS + m, u)
                    if start and u == 2:
                        fill(0)
                        fill(1)
                    if start and 3 <= u <= 7:
                        fill(u - 1)
                    if prev and u == 6:
                        leaky(h1, bias1_set, m - 1, h1_set)
                    if prev and u == 9:
                        leaky(h2, bias2_set, m - 1, h2_set)
                    if prev and u == 12:
                        features(m - 1, prev_c, mlp)
                    if start and u == 13:
                        fill(7)

            def a_round(r, mlp, prev_mlp):
                m = r * CHUNKS
                passing(m, 0, prev_mlp, prev_mlp is not None, True, r, CHUNKS - 1)
                with dve.Fori(1, CHUNKS) as c:
                    passing(m + c, c, mlp, True, False, r, c - 1)

            a_round(0, uv, None)
            with dve.Fori(0, (ROUNDS - 1) // 2) as q:
                a_round(2 * q + 1, vu, uv)
                a_round(2 * q + 2, uv, vu)
            m = ROUNDS * CHUNKS - 1
            leaky(h1, bias1_set, m, h1_set)
            leaky(h2, bias2_set, m, h2_set)
            features(m, CHUNKS - 1, uv)
            for c in range(CHUNKS):
                cols = slice(c * COLS, (c + 1) * COLS)
                dve.wait_ge(fresh, (ROUNDS - 1) * CHUNKS + c + 1)
                dve.tensor_tensor(stage[:, cols], stage[:, cols], x_sb[:, cols], ALU.add).then_inc(final, 1)

        @block.tensor
        def _(pe):
            pe.wait_ge(params_in_sb, 16)
            pe.wait_ge(ones_set, 1)
            w0 = params[:, W0:W0 + P]
            with pe.Fori(0, CHUNKS) as c:
                pe.wait_ge(first["done"], c + 1)
                pe.wait_ge(pre_y, c)
                for b in range(PER):
                    mm = pe.transpose(tp[:, b * P:(b + 1) * P], h2[:, b * P:(b + 1) * P], ident)
                mm.then_inc(pre_t, 1)
                pe.wait_ge(pre_y, c + 1)
                pe.wait_ge(pre_h1, c)
                pe.matmul(z1, w0, y[:, :], start=True, stop=True).then_inc(pre_hwt, 1)
                pe.wait_ge(pre_st, c)
                for b in range(PER):
                    mm = pe.matmul(z2[:, b * P:(b + 1) * P], y[:, b * P:(b + 1) * P], w0, start=True, stop=True)
                mm.then_inc(pre_hw, 1)
                pe.wait_ge(pre_h1, c + 1)
                pe.wait_ge(pre_pc, c)
                for b in range(PER):
                    mm = pe.matmul(tiny[:, 2 * b:2 * b + 2], h1[:, b * P:(b + 1) * P], a12, start=True, stop=True)
                mm.then_inc(pre_p, 1)

            def e_turn(c):
                pe.wait_ge(params_in_sb, 16)
                pe.wait_ge(e_row, c + 1)
                wait(pe, e_col, c)
                for b in range(PER):
                    mm = pe.transpose(tiny[:, 8 * b:8 * b + 7], y[0:7, b * P:(b + 1) * P], ident[0:7, 0:7])
                mm.then_inc(e_turned, 1)

            def e_chunk(c, par, prev):
                wait(pe, e_row, c - 1)
                for u in range(UNITS):
                    pe.wait_ge(masked, c * UNITS + u + 1)
                    for b in range(UB):
                        j = u * UB + b
                        for g in range(2):
                            mm = pe.matmul(row[par][0:7, :], probe[:, j, 7 * g:7 * g + 7],
                                           masks[:, u % SPLIT, g, b * COLS:(b + 1) * COLS],
                                           start=(j == 0 and g == 0), stop=(j == BLOCKS - 1 and g == 1))
                    mm.then_inc(mask_used, 1)
                    if prev and u == 3:
                        e_turn(c - 1)

            pe.wait_ge(probe_set, 1)
            for par in range(2):
                e_chunk(par, par, par == 1)
            with pe.Fori(1, CHUNKS // 2) as k:
                for par in range(2):
                    e_chunk(2 * k + par, par, True)
            e_turn(CHUNKS - 1)

            def products(m_abs, par, u, stationary_ready, sums):
                v = m_abs * UNITS + u
                pe.wait_ge(hi_set, v + 1)
                pe.wait_ge(lo_set, v + 1)
                if sums:
                    pe.wait_ge(pos_set, v + 1)
                for b in range(UB):
                    j = u * UB + b
                    stationary_ready(j)
                    cols, mov = slice(j * P, (j + 1) * P), slice(b * COLS, (b + 1) * COLS)
                    hi, lo = a_hi[:, u % SPLIT, mov], a_lo[:, u % SPLIT, mov]
                    if sums:
                        pe.matmul(row[par][0:3, :], wpart[:, j, :], pos[:, u % 2, mov],
                                  start=(j == 0), stop=(j == BLOCKS - 1))
                    pe.matmul(acc[par], u_hi[:, cols], hi, start=(j == 0), stop=False)
                    pe.matmul(acc[par], u_hi[:, cols], lo, start=False, stop=False)
                    mm = pe.matmul(acc[par], u_lo[:, cols], hi, start=False, stop=(j == BLOCKS - 1))
                mm.then_inc(unit_used, 1)

            def turn(n, s):
                pe.wait_ge(s["copied"], n + 1)
                wait(pe, s["done"], n)
                for b in range(PER):
                    pe.transpose(tp[:, b * P:(b + 1) * P], y[:, b * P:(b + 1) * P], ident)
                for b in range(PER):
                    mm = pe.transpose(tiny[:, 4 * b:4 * b + 3], h2[0:3, b * P:(b + 1) * P], ident[0:3, 0:3])
                mm.then_inc(s["turned"], 1)

            def attention(c, par, prev):
                wait(pe, fast["copied"], c - 1)
                for u in range(UNITS):
                    def ready(j):
                        if isinstance(c, int) and c == 0:
                            pe.wait_ge(u_lo_set, j + 1)
                    products(c, par, u, ready, True)
                    if prev and u == 5:
                        turn(c - 1, fast)

            pe.wait_ge(w_set, 1)
            attention(0, 0, False)
            attention(1, 1, True)
            with pe.Fori(1, CHUNKS // 2) as k:
                for par in range(2):
                    attention(2 * k + par, par, True)
            turn(CHUNKS - 1, fast)

            pe.wait_ge(bad_set, 1)
            pe.matmul(tiny[:, 0:1], ones[:, :], bad[:, 1:2], start=True, stop=True).then_inc(bad_sum, 1)
            pe.wait_ge(flag_set, 1)
            with pe.If(pe.value_load(flag[0:1, 0:1], min_val=0, max_val=P) != 0):
                def tile(c, u, b, begin, end):
                    n = c * BLOCKS + u * UB + b
                    pe.wait_ge(hw_landed[b], c * (UNITS * 16) + u * 16 + 16)
                    pe.wait_ge(g_tile, n + 1)
                    pe.matmul(acc[0], g_hw[b], g_num, start=begin, stop=end)
                    pe.matmul(row[0][0:3, :], pick[:, :], g_den, start=begin, stop=end).then_inc(g_prod, 1)

                with pe.Fori(0, CHUNKS) as c:
                    tile(c, 0, 0, True, False)
                    tile(c, 0, 1, False, False)
                    with pe.Fori(1, UNITS - 1) as u:
                        tile(c, u, 0, False, False)
                        tile(c, u, 1, False, False)
                    tile(c, UNITS - 1, 0, False, False)
                    tile(c, UNITS - 1, 1, False, True)
                    turn(c, slow)

            def mlp1(m, mlp):
                pe.wait_ge(y_set, m + 1)
                wait(pe, bias1_set, m)
                pe.matmul(z1, mlp.w[0], y[:, :], start=True, stop=True).then_inc(z1_set, 1)

            def mlp2(m, mlp):
                pe.wait_ge(h1_set, m + 1)
                wait(pe, bias2_set, m)
                pe.matmul(z2, mlp.w[1], h1[:, :], start=True, stop=True).then_inc(z2_set, 1)

            def mlp3(m, mlp):
                pe.wait_ge(h2_set, m + 1)
                wait(pe, t3_set, m)
                for b in range(PER):
                    mm = pe.matmul(tp[:, b * P:(b + 1) * P], h2[:, b * P:(b + 1) * P], mlp.w[2],
                                   start=True, stop=True)
                mm.then_inc(z3_set, 1)

            def passing(m, par, mlp, prev, start, r):
                wait(pe, y_set, m - 1)
                for u in range(UNITS):
                    def ready(j):
                        if start and j % PER == 0:
                            pe.wait_ge(u_lo_set, BLOCKS + r * CHUNKS + j // PER + 1)
                    products(CHUNKS + m, par, u, ready, False)
                    if prev and u == 1:
                        mlp1(m - 1, mlp)
                    if prev and u == 4:
                        mlp2(m - 1, mlp)
                    if prev and u == 8:
                        mlp3(m - 1, mlp)

            def a_round(r, mlp, prev_mlp):
                m = r * CHUNKS
                passing(m, 0, prev_mlp, prev_mlp is not None, True, r)
                passing(m + 1, 1, mlp, True, False, r)
                with pe.Fori(1, CHUNKS // 2) as k:
                    for par in range(2):
                        passing(m + 2 * k + par, par, mlp, True, False, r)

            a_round(0, uv, None)
            with pe.Fori(0, (ROUNDS - 1) // 2) as q:
                a_round(2 * q + 1, vu, uv)
                a_round(2 * q + 2, uv, vu)
            m = ROUNDS * CHUNKS - 1
            mlp1(m, uv)
            mlp2(m, uv)
            mlp3(m, uv)


def kernel(x, adj, L0_gnn_W, L0_gnn_a, L1_gnn_v_node_feats, L1_gnn_uv_W1, L1_gnn_uv_b1, L1_gnn_uv_W2,
           L1_gnn_uv_b2, L1_gnn_uv_W3, L1_gnn_uv_b3, L1_gnn_vu_W1, L1_gnn_vu_b1, L1_gnn_vu_W2,
           L1_gnn_vu_b2, L1_gnn_vu_W3, L1_gnn_vu_b3):
    import numpy as np
    import concourse.bacc as bacc
    from concourse.bass_utils import run_bass_kernel_spmd

    a = np.asarray(adj).reshape(P, CHUNKS, PER, P, UNITS, UB).transpose(1, 4, 3, 5, 2, 0)
    a = np.ascontiguousarray(a).reshape(CHUNKS * UNITS, P, UW)
    rows = [np.broadcast_to(np.asarray(b)[None, :], (P, P)) for b in (L1_gnn_uv_b3, L1_gnn_vu_b3)]
    columns = [np.asarray(b)[:, None] for b in (L1_gnn_uv_b1, L1_gnn_uv_b2, L1_gnn_vu_b1, L1_gnn_vu_b2)]
    halves = np.asarray(L0_gnn_a).reshape(2, P).transpose()
    params = np.concatenate(
        [np.asarray(w) for w in (L0_gnn_W, L1_gnn_uv_W1, L1_gnn_uv_W2, L1_gnn_uv_W3, L1_gnn_vu_W1,
                                 L1_gnn_vu_W2, L1_gnn_vu_W3)]
        + rows + [np.eye(P, dtype=np.float32), halves] + columns, axis=1)
    arrays = {"x_in": np.ascontiguousarray(np.asarray(x)).reshape(P, N), "adj_in": a,
              "params_in": np.ascontiguousarray(params)}

    nc = bacc.Bacc("TRN2", target_bir_lowering=False, num_devices=1)
    ins = {k: nc.dram_tensor(k, v.shape, F32, kind="ExternalInput").ap() for k, v in arrays.items()}
    out = nc.dram_tensor("out", (P, N), F32, kind="ExternalOutput").ap()
    hw_dram = nc.dram_tensor("hw_dram", (P, N), F32, kind="Internal").ap()
    build(nc, ins["x_in"], ins["adj_in"], ins["params_in"], out, hw_dram)
    got = run_bass_kernel_spmd(nc, [arrays], core_ids=[0])
    return np.asarray(got.results[0]["out"]).reshape(N, P)
```

```python
from contextlib import ExitStack

import concourse.bass as bass
from concourse import mybir

P = 128
N = 4096
BLOCKS = N // P
COLS = 512
CHUNKS = N // COLS
PER = COLS // P
UB = 2
UNITS = BLOCKS // UB
UW = UB * COLS
KEPT = 2
RING = 7
STREAMED = UNITS - KEPT
LAPS = STREAMED // RING
SPLIT = 4
ROUNDS = 5
EPS = 1e-5
SLOPE = 0.01
E_SLOPE = 0.2
TOP = 75.0
LEAST = 1e-30
HUGE = 3.0e38
TINY = 1e-37

F32 = mybir.dt.float32
F32R = mybir.dt.float32r
BF16 = mybir.dt.bfloat16
I32 = mybir.dt.int32
ALU = mybir.AluOpType
ACT = mybir.ActivationFunctionType
AX = mybir.AxisListType
RMAX = bass.bass_isa.ReduceOp.max

W0, UV, VU, B3UV, B3VU, IDENT, A12, BIAS = 0, 128, 512, 896, 1024, 1152, 1280, 1282
PARAMS = 1286
G_LINKS = 2 + BLOCKS * (5 + 3)
ROOT_LINKS = 5
MERGE_LINKS = 4 + 1 + 2 + ROOT_LINKS + 1


def build(nc, x_in, adj, params_in, out, hw_dram):
    assert STREAMED % RING == 0 and UNITS % SPLIT == 0
    ctx = ExitStack()
    with ctx:
        def sb(name, shape, dt):
            return ctx.enter_context(nc.sbuf_tensor(name, shape, dt))

        def sem(name):
            return ctx.enter_context(nc.semaphore(name))

        params = sb("params", [P, PARAMS], F32)
        x_sb = sb("x_sb", [P, N], F32)
        stage = sb("stage", [P, N], F32)
        u_hi = sb("u_hi", [P, N], F32R)
        scratch_at = nc.sbuf_base
        u_lo = sb("u_lo", [P, N], F32R)
        scratch = nc.alloc_sbuf_tensor_at("scratch", [P, N], F32, offset=scratch_at)
        kept = sb("kept", [P, CHUNKS, KEPT * UW], F32)
        ring = sb("ring", [P, RING, UW], F32)
        a_hi = sb("a_hi", [P, SPLIT, UW], F32R)
        early_at = nc.sbuf_base
        a_lo = sb("a_lo", [P, SPLIT, UW], F32R)
        probe = nc.alloc_sbuf_tensor_at("probe", [P, BLOCKS, 14], BF16, offset=early_at)
        early = nc.alloc_sbuf_tensor_at("early", [P, 26 * BLOCKS], F32, offset=early_at + 28 * BLOCKS)
        pos2 = sb("pos2", [P, 2, UW], BF16)
        y = sb("y", [P, COLS], F32)
        h1 = sb("h1", [P, COLS], F32)
        h2 = sb("h2", [P, COLS], F32)
        wpart = sb("wpart", [P, BLOCKS, 32], BF16)
        e_pm = sb("e_pm", [P, BLOCKS, 2], F32)
        w_all = sb("w_all", [P, BLOCKS], F32)
        den_all = sb("den_all", [P, BLOCKS], F32)
        var_all = sb("var_all", [P, BLOCKS], F32)
        bad = sb("bad", [P, 4], F32)
        flag = sb("flag", [P, 1], I32)
        top = sb("top", [P, 2], F32)
        stats = sb("stats", [P, PER, 6], F32)
        mv = sb("mv", [P, PER, 2], F32)
        small = sb("small", [P, 8, PER], F32)
        ok_all = sb("ok_all", [P, BLOCKS], F32)
        noneg = sb("noneg", [P, BLOCKS], F32)
        gate = sb("gate", [P, 6], F32)
        pick = sb("pick", [P, P], F32)
        psum = ctx.enter_context(nc.psum_tensor("psum", [P, 8, COLS], F32))
        acc = [psum[:, 0, :], psum[:, 1, :]]
        row = [psum[:, 2, :], psum[:, 3, :]]
        z1, z2, tp, tiny = (psum[:, k, :] for k in (4, 5, 6, 7))

        pos = [pos2[:, 0, :], pos2[:, 1, :], stage[:, N - COLS:].bitcast(BF16), h1[:, :].bitcast(BF16)]
        ident = params[:, IDENT:IDENT + P]
        a12 = params[:, A12:A12 + 2]
        masks = scratch[:, :].bitcast(BF16).rearrange("p (s g c) -> p s g c", s=SPLIT, g=2)
        fb = scratch[:, :].rearrange("p (k c) -> p k c", c=COLS)
        g_a = [fb[:, 0, :], fb[:, 1, :]]
        g_row, g_neg, g_t, g_e, g_num, g_den = (fb[:, k, :] for k in range(2, 8))
        g_s = h1[:, :]
        g_hw = [h2[:, 0:P], h2[:, P:2 * P]]
        e_plus, e_minus = e_pm[:, :, 0], e_pm[:, :, 1]
        def early_part(at, k):
            return early[:, at * BLOCKS:(at + k) * BLOCKS].rearrange("p (b k) -> p b k", k=k)

        stats0, mv0 = early_part(0, 6), early_part(6, 2)
        root0 = early[:, 8 * BLOCKS:15 * BLOCKS].rearrange("p (k b) -> p k b", k=7)
        p_all = early_part(15, 2)
        rest = early_part(17, 2)
        e_all = early_part(19, 7)
        e_sum = early_part(0, 2)

        class Mlp:
            def __init__(self, at, b3, b):
                self.w = [params[:, at + k * P:at + (k + 1) * P] for k in range(3)]
                self.b1, self.b2 = params[:, BIAS + b:BIAS + b + 1], params[:, BIAS + b + 1:BIAS + b + 2]
                self.b3 = params[:, b3:b3 + P].unsqueeze(1).broadcast_to([P, PER, P])

        uv, vu = Mlp(UV, B3UV, 0), Mlp(VU, B3VU, 2)

        params_in_sb, kept_in = sem("params_in_sb"), sem("kept_in")
        x_in_sb = [sem(f"x_in_sb{q}") for q in range(4)]
        landed = [sem(f"landed{s}") for s in range(RING)]
        hw_out, hw_done, out_done = sem("hw_out"), sem("hw_done"), sem("out_done")
        pick_set = sem("pick_set")

        def norm_sems(tag):
            return {k: sem(f"{tag}_{k}") for k in ("chain", "var", "std", "done")}

        first = norm_sems("first")
        pre_t, pre_y, pre_hwt, pre_h1, pre_hw, pre_st, pre_p, pre_pc = (
            sem(f"pre_{k}") for k in ("turned", "y", "hwt", "h1", "hw", "stage", "p", "pcopied"))
        masked, mask_used = sem("masked"), sem("mask_used")
        e_row, e_turned, e_col = sem("e_row"), sem("e_turned"), sem("e_col")
        chain = sem("chain")
        probe_set, top_part, top_all, shifted, w_exp, w_set = (
            sem(k) for k in ("probe_set", "top_part", "top_all", "shifted", "w_exp", "w_set"))
        u_hi_set, u_lo_set = sem("u_hi_set"), sem("u_lo_set")
        hi_set, lo_set, unit_used = sem("hi_set"), sem("lo_set"), sem("unit_used")
        pos_even, pos_odd = sem("pos_even"), sem("pos_odd")
        bias1_set, bias2_set = sem("bias1_set"), sem("bias2_set")
        y_set, z1_set, h1_set, z2_set, h2_set, z3_set, t3_set, fresh = (
            sem(k) for k in ("y_set", "z1_set", "h1_set", "z2_set", "h2_set", "z3_set", "t3_set", "fresh"))

        def merge_sems(tag):
            got = norm_sems(tag)
            got.update({k: sem(f"{tag}_{k}") for k in ("copied", "turned")})
            got["primed"] = int(tag == "slow")
            return got

        fast, slow = merge_sems("fast"), merge_sems("slow")
        bad_set, bad_sum, flag_set = sem("bad_set"), sem("bad_sum"), sem("flag_set")
        final = sem("final")
        g_landed = [sem("g_landed0"), sem("g_landed1")]
        hw_landed = [sem("hw_landed0"), sem("hw_landed1")]
        g_noneg = sem("g_noneg")
        g_x, g_freed, g_chain, g_all, g_arg, g_exp, g_tile, g_prod = (
            sem(f"g_{k}") for k in ("x", "freed", "chain", "all", "arg", "exp", "tile", "prod"))

        block = ctx.enter_context(nc.Block())

        def wait(eng, s, value):
            if not isinstance(value, int) or value > 0:
                eng.wait_ge(s, value)

        class Link:

            def __init__(self, s, base=0):
                self.s, self.base, self.k = s, base, 0

            def __call__(self, ins, gated=False):
                self.k += 1
                ins.then_inc(self.s, 1)
                nc.vector.wait_ge(self.s, self.base + self.k)
                if gated:
                    nc.vector.memset(gate[:, 0:1], 0.0)

        def chunk_cols(c):
            return bass.ds(c * COLS, COLS) if not isinstance(c, int) else slice(c * COLS, (c + 1) * COLS)

        def unit_raw(c, u):
            return kept[:, c, u * UW:(u + 1) * UW] if u < KEPT else ring[:, (u - KEPT) % RING, :]

        def wait_raw(eng, t, u):
            if u >= KEPT:
                n = u - KEPT
                eng.wait_ge(landed[n % RING], 16 * (LAPS * t + n // RING + 1))

        A_PASS, M_PASS = CHUNKS, 2 * CHUNKS

        @block.sync
        def _(sp):
            def load(c, u, n):
                sp.dma_start(ring[:, n % RING, :], adj[c * UNITS + u]).then_inc(landed[n % RING], 16)

            sp.dma_start(params[:, :], params_in).then_inc(params_in_sb, 16)
            for q in range(4):
                sp.dma_start(x_sb[:, q * 1024:(q + 1) * 1024],
                             x_in[:, q * 1024:(q + 1) * 1024]).then_inc(x_in_sb[q], 16)
            for c in range(CHUNKS):
                for k in range(KEPT):
                    sp.dma_start(kept[:, c, k * UW:(k + 1) * UW], adj[c * UNITS + k]).then_inc(kept_in, 16)

            def first_pass(c):
                for n in range(STREAMED):
                    wait(sp, masked, c * UNITS + n + KEPT - RING + 1 if n >= RING
                         else (c - 1) * UNITS + n + KEPT + RING + 1)
                    load(c, n + KEPT, n)

            def later(c, t, since, n):
                v = (t - A_PASS) * UNITS + n + KEPT - RING + 1 if n >= RING \
                    else (t - A_PASS - 1) * UNITS + n + KEPT + RING + 1
                if since == 0 and n < RING:
                    sp.wait_ge(masked, CHUNKS * UNITS)
                else:
                    sp.wait_ge(hi_set, v)
                    sp.wait_ge(lo_set, v)
                load(c, n + KEPT, n)

            first_pass(0)
            with sp.Fori(1, CHUNKS) as c:
                first_pass(c)
            for n in range(STREAMED):
                later(0, A_PASS, 0, n)
            with sp.Fori(1, CHUNKS) as c:
                for n in range(STREAMED):
                    later(c, A_PASS + c, 1, n)
            for n in range(RING):
                later(0, M_PASS, 1, n)

            sp.wait_ge(flag_set, 1)
            sp.wait_ge(hw_done, 16)
            with sp.If(sp.value_load(flag[0:1, 0:1], min_val=0, max_val=P) != 0):
                sp.dma_start(stage[:, :], x_in).then_inc(g_x, 16)
                with sp.Fori(0, CHUNKS) as c:
                    for phase in range(2):
                        with sp.Fori(0, UNITS) as u:
                            for b in range(UB):
                                m = (c * 2 + phase) * BLOCKS + u * UB
                                sp.wait_ge(g_freed, m + 1)
                                if phase:
                                    sp.wait_ge(g_prod, c * BLOCKS + u * UB + 1)
                                    sp.dma_start(g_hw[b], hw_dram[:, bass.ds(u * (UB * P) + b * P, P)]) \
                                        .then_inc(hw_landed[b], 16)
                                sp.dma_start(g_a[b], adj[c * UNITS + u][:, b * COLS:(b + 1) * COLS]) \
                                    .then_inc(g_landed[b], 16)

            for n in range(RING, STREAMED):
                later(0, M_PASS, 1, n)
            with sp.Fori(1, CHUNKS) as c:
                for n in range(STREAMED):
                    later(c, M_PASS + c, 1, n)
            with sp.Fori(1, ROUNDS) as r:
                with sp.Fori(0, CHUNKS) as c:
                    for n in range(STREAMED):
                        later(c, M_PASS + r * CHUNKS + c, 1, n)
            for c in range(CHUNKS):
                sp.wait_ge(final, c + 1)
                sp.dma_start(out[:, c * COLS:(c + 1) * COLS], stage[:, c * COLS:(c + 1) * COLS]) \
                    .then_inc(out_done, 16)
            sp.wait_ge(out_done, 16 * CHUNKS)

        @block.gpsimd
        def _(pool):
            nc.gpsimd.memset(pick[:, 0:1], 1.0)
            nc.gpsimd.memset(pick[:, 1:P], 0.0).then_inc(pick_set, 1)
            pool.wait_ge(top_part, 1)
            nc.gpsimd.partition_all_reduce(top[:, 1:2], top[:, 0:1], P, RMAX).then_inc(top_all, 1)
            pool.wait_ge(flag_set, 1)
            with pool.If(pool.value_load(flag[0:1, 0:1], min_val=0, max_val=P) != 0):
                with pool.Fori(0, CHUNKS) as c:
                    pool.wait_ge(g_freed, (2 * c + 1) * BLOCKS + 1)
                    nc.gpsimd.tensor_tensor(gate[:, 1:2], pick[:, 0:1], pick[:, 1:2], ALU.mult)
                    nc.gpsimd.partition_all_reduce(g_e, g_row, P, RMAX).then_inc(g_all, 1)

        @block.scalar
        def _(act):
            act.wait_ge(first["var"], 1)
            act.activation(root0[:, 1, :], root0[:, 0, :], ACT.Sqrt).then_inc(first["std"], 1)

            def project(c):
                act.wait_ge(pre_t, c + 1)
                wait(act, pre_hw, c)
                act.activation(y[:, :], tp, ACT.Copy).then_inc(pre_y, 1)
                act.wait_ge(pre_hwt, c + 1)
                wait(act, pre_p, c)
                act.activation(h1[:, :], z1, ACT.Copy).then_inc(pre_h1, 1)

            project(0)
            with act.Fori(1, CHUNKS) as c:
                project(c)
            act.wait_ge(pre_st, CHUNKS)
            act.dma_start(hw_dram, stage[:, :]).then_inc(hw_done, 16)

            def e_copy(c, par):
                act.wait_ge(mask_used, (c + 1) * UNITS)
                wait(act, e_turned, c)
                act.activation(y[0:7, :], row[par][0:7, :], ACT.Copy).then_inc(e_row, 1)

            e_copy(0, 0)
            e_copy(1, 1)
            with act.Fori(1, CHUNKS // 2) as k:
                for par in range(2):
                    e_copy(2 * k + par, par)

            act.wait_ge(shifted, 1)
            act.activation(w_all[:, :], e_sum[:, :, 0], ACT.Exp).then_inc(w_exp, 1)
            act.wait_ge(w_exp, 1)
            for b in range(BLOCKS):
                act.activation(u_hi[:, b * P:(b + 1) * P], stage[:, b * P:(b + 1) * P], ACT.Copy,
                               scale=w_all[:, b:b + 1]).then_inc(u_hi_set, 1)

            def split_hi(c, t, u):
                v = (t - A_PASS) * UNITS + u
                wait_raw(act, t, u)
                wait(act, unit_used, v - SPLIT + 1)
                act.activation(a_hi[:, u % SPLIT, :], unit_raw(c, u), ACT.Copy).then_inc(hi_set, 1)

            def merge_copy(n, s, num, den):
                if s is fast:
                    act.wait_ge(unit_used, (n + 1) * UNITS)
                else:
                    act.wait_ge(g_prod, (n + 1) * BLOCKS + 1)
                wait(act, s["turned"], n + s["primed"])
                act.activation(y[:, :], num, ACT.Copy)
                act.activation(h2[:, :], den, ACT.Copy).then_inc(s["copied"], 1)

            def merge_root(n, s):
                act.wait_ge(s["var"], n + 1)
                act.activation(small[:, 1, :], small[:, 0, :], ACT.Sqrt).then_inc(s["std"], 1)

            def attention(c, par, prev):
                for u in range(UNITS):
                    def mask():
                        act.activation(pos[u % SPLIT], unit_raw(c, u), ACT.Sign).then_inc(pos_odd, 1)

                    if u % 2 and u >= KEPT:
                        wait_raw(act, A_PASS + c, u)
                        wait(act, unit_used, c * UNITS + u - SPLIT + 1)
                        mask()
                    split_hi(c, A_PASS + c, u)
                    if u % 2 and u < KEPT:
                        mask()
                    if prev and u == 3:
                        merge_copy(c - 1, fast, acc[1 - par], row[1 - par])
                    if prev and u == 8:
                        merge_root(c - 1, fast)

            act.wait_ge(kept_in, 16 * CHUNKS * KEPT)
            attention(0, 0, False)
            attention(1, 1, True)
            with act.Fori(1, CHUNKS // 2) as k:
                for par in range(2):
                    attention(2 * k + par, par, True)
            merge_copy(CHUNKS - 1, fast, acc[1], row[1])
            merge_root(CHUNKS - 1, fast)

            act.wait_ge(flag_set, 1)
            with act.If(act.value_load(flag[0:1, 0:1], min_val=0, max_val=P) != 0):
                with act.Fori(0, CHUNKS) as c:
                    with act.Fori(0, BLOCKS) as j:
                        for s in range(2):
                            act.wait_ge(g_arg, c * (2 * BLOCKS) + j * 2 + s + 1)
                            act.activation(g_e, g_t, ACT.Exp).then_inc(g_exp, 1)
                    merge_copy(c, slow, acc[0], row[0])
                    merge_root(c, slow)
                act.wait_ge(slow["done"], CHUNKS + 1)

            def y_copy(m, par):
                act.wait_ge(unit_used, (CHUNKS + m + 1) * UNITS)
                wait(act, z1_set, m)
                act.activation(y[:, :], acc[par], ACT.Copy).then_inc(y_set, 1)

            def bias1(m, mlp):
                act.wait_ge(z1_set, m + 1)
                wait(act, fresh, m)
                act.activation(h1[:, :], z1, ACT.Identity, bias=mlp.b1).then_inc(bias1_set, 1)

            def bias2(m, mlp):
                act.wait_ge(z2_set, m + 1)
                wait(act, z3_set, m)
                act.activation(h2[:, :], z2, ACT.Identity, bias=mlp.b2).then_inc(bias2_set, 1)

            def fill_hi(m, s):
                act.activation(u_hi[:, s * COLS:(s + 1) * COLS], stage[:, s * COLS:(s + 1) * COLS],
                               ACT.Copy).then_inc(u_hi_set, 1)

            def passing(m, c, par, mlp, prev, start):
                for u in range(UNITS):
                    split_hi(c, M_PASS + m, u)
                    if prev and u == 2:
                        y_copy(m - 1, 1 - par)
                    if start and u == 2:
                        act.wait_ge(unit_used, (CHUNKS + m) * UNITS)
                        wait(act, fresh, m - 1)
                        fill_hi(m, 0)
                        fill_hi(m, 1)
                    if start and 3 <= u <= 7:
                        fill_hi(m, u - 1)
                    if prev and u == 5:
                        bias1(m - 1, mlp)
                    if prev and u == 8:
                        bias2(m - 1, mlp)
                    if start and u == 12:
                        wait(act, fresh, m)
                        fill_hi(m, 7)

            def a_round(r, mlp, prev_mlp):
                m = r * CHUNKS
                passing(m, 0, 0, prev_mlp, prev_mlp is not None, True)
                passing(m + 1, 1, 1, mlp, True, False)
                with act.Fori(1, CHUNKS // 2) as k:
                    for par in range(2):
                        passing(m + 2 * k + par, 2 * k + par, par, mlp, True, False)

            act.wait_ge(fast["done"], CHUNKS)
            a_round(0, uv, None)
            with act.Fori(0, (ROUNDS - 1) // 2) as q:
                a_round(2 * q + 1, vu, uv)
                a_round(2 * q + 2, uv, vu)
            m = ROUNDS * CHUNKS - 1
            y_copy(m, 1)
            bias1(m, uv)
            bias2(m, uv)

        @block.vector
        def _(dve):
            def root(tile, links, s, n):
                dve.wait_ge(s["std"], n + 1)
                links(dve.reciprocal(tile[:, 2, :], tile[:, 1, :]))
                links(dve.tensor_tensor(tile[:, 3, :], tile[:, 2, :], tile[:, 2, :], ALU.mult))
                links(dve.tensor_tensor(tile[:, 4, :], tile[:, 3, :], tile[:, 0, :], ALU.mult))
                links(dve.tensor_scalar(tile[:, 5, :], tile[:, 4, :], -0.5, 1.5, ALU.mult, ALU.add))
                links(dve.tensor_tensor(tile[:, 6, :], tile[:, 5, :], tile[:, 2, :], ALU.mult))

            link = Link(chain)
            for b in range(BLOCKS):
                if b % (BLOCKS // 4) == 0:
                    dve.wait_ge(x_in_sb[b // (BLOCKS // 4)], 16)
                ins = dve.bn_stats(stats0[:, b, :], x_sb[:, b * P:(b + 1) * P])
            link(ins)
            for b in range(BLOCKS):
                ins = dve.bn_aggr(mv0[:, b, :], stats0[:, b, :])
            link(ins)
            dve.tensor_scalar(root0[:, 0, :], mv0[:, :, 1], EPS, None, ALU.add).then_inc(first["var"], 1)
            root(root0, link, first, 0)
            link(dve.tensor_tensor(root0[:, 5, :], mv0[:, :, 0], root0[:, 6, :], ALU.mult))

            def normalise(c):
                cols = bass.ds(c * PER, PER) if not isinstance(c, int) else slice(c * PER, (c + 1) * PER)

                def wide(k):
                    return root0[:, k, cols].unsqueeze(2).broadcast_to([P, PER, P])

                wait(dve, pre_t, c)
                blocks = h2[:, :].rearrange("p (b f) -> p b f", b=PER)
                dve.tensor_tensor(blocks, x_sb[:, chunk_cols(c)].rearrange("p (b f) -> p b f", b=PER),
                                  wide(6), ALU.mult).then_inc(first["chain"], 1)
                dve.wait_ge(first["chain"], 2 * c + 1)
                dve.tensor_tensor(blocks, blocks, wide(5), ALU.subtract).then_inc(first["chain"], 1)
                dve.wait_ge(first["chain"], 2 * c + 2)
                dve.tensor_scalar(h2[:, :], h2[:, :], 0.0, None, ALU.max).then_inc(first["done"], 1)

            def keep(c):
                cols = bass.ds(c * PER, PER) if not isinstance(c, int) else slice(c * PER, (c + 1) * PER)
                dve.wait_ge(pre_hw, c + 1)
                dve.tensor_copy(stage[:, chunk_cols(c)], z2).then_inc(pre_st, 1)
                dve.wait_ge(pre_p, c + 1)
                dve.tensor_copy(p_all[:, cols, :],
                                tiny[:, 0:2 * PER].rearrange("p (b k) -> p b k", k=2)).then_inc(pre_pc, 1)

            normalise(0)
            with dve.Fori(1, CHUNKS) as c:
                normalise(c)
                keep(c - 1)
            keep(CHUNKS - 1)

            dve.wait_ge(pre_pc, CHUNKS)
            dve.memset(wpart[:, :, :], 0.0)
            link(dve.memset(probe[:, :, :], 0.0))
            dve.memset(probe[:, :, 13], 1.0)
            source = p_all
            for part in range(3):
                for k in range(2):
                    ins = dve.tensor_copy(probe[:, :, 3 * k + part], source[:, :, k])
                link(ins)
                for k in range(2):
                    ins = dve.tensor_copy(probe[:, :, 10 - 3 * k + part], source[:, :, k])
                    if part < 2:
                        ins = dve.tensor_tensor(rest[:, :, k], source[:, :, k], probe[:, :, 3 * k + part],
                                                ALU.subtract)
                if part < 2:
                    link(ins)
                source = rest
            ins.then_inc(probe_set, 1)

            def e_cols(c):
                dve.wait_ge(e_turned, c + 1)
                cols = bass.ds(c * PER, PER) if not isinstance(c, int) else slice(c * PER, (c + 1) * PER)
                dve.tensor_copy(e_all[:, cols, :],
                                tiny[:, 0:8 * PER].rearrange("p (b k) -> p b k", k=8)[:, :, 0:7]) \
                    .then_inc(e_col, 1)

            def mask_chunk(c, prev):
                for u in range(UNITS):
                    wait_raw(dve, c, u)
                    wait(dve, mask_used, c * UNITS + u - SPLIT + 1)
                    dve.tensor_scalar(masks[:, u % SPLIT, 0, :], unit_raw(c, u), 0.0, None, ALU.is_gt)
                    dve.tensor_scalar(masks[:, u % SPLIT, 1, :], unit_raw(c, u), 0.0, None, ALU.is_lt) \
                        .then_inc(masked, 1)
                    if prev and u == 6:
                        e_cols(c - 1)

            dve.wait_ge(kept_in, 16 * CHUNKS * KEPT)
            mask_chunk(0, False)
            with dve.Fori(1, CHUNKS) as c:
                mask_chunk(c, True)
            e_cols(CHUNKS - 1)

            dve.wait_ge(e_col, CHUNKS)
            for k in range(2):
                ins = dve.tensor_reduce(e_sum[:, :, k], e_all[:, :, 3 * k:3 * k + 3], AX.X, ALU.add)
            link(ins)
            link(dve.scalar_tensor_tensor(out=e_pm[:, :, :], in0=e_sum[:, :, :], scalar=E_SLOPE, in1=e_sum[:, :, :],
                                          op0=ALU.mult, op1=ALU.max))
            dve.tensor_reduce(top[:, 0:1], e_plus, AX.X, ALU.max).then_inc(top_part, 1)
            dve.tensor_scalar(noneg[:, :], e_all[:, :, 6], 0.5, None, ALU.is_lt)
            dve.wait_ge(top_all, 1)
            dve.tensor_scalar(e_sum[:, :, 0], e_plus, top[:, 1:2], TOP, ALU.subtract, ALU.add) \
                .then_inc(shifted, 1)
            dve.wait_ge(w_exp, 1)
            source = w_all
            for part in range(3):
                ins = dve.tensor_copy(wpart[:, :, part], source[:, :])
                if part < 2:
                    link(ins)
                    link(dve.tensor_tensor(rest[:, :, 0], source[:, :], wpart[:, :, part], ALU.subtract))
                    source = rest[:, :, 0]
            ins.then_inc(w_set, 1)
            dve.wait_ge(mask_used, CHUNKS * UNITS)
            for b in range(BLOCKS):
                cols = slice(b * P, (b + 1) * P)
                dve.wait_ge(u_hi_set, b + 1)
                dve.scalar_tensor_tensor(out=u_lo[:, cols], in0=stage[:, cols], scalar=w_all[:, b:b + 1],
                                         in1=u_hi[:, cols].bitcast(F32), op0=ALU.mult, op1=ALU.subtract) \
                    .then_inc(u_lo_set, 1)

            def split_lo(c, t, u):
                dve.wait_ge(hi_set, (t - A_PASS) * UNITS + u + 1)
                dve.tensor_tensor(a_lo[:, u % SPLIT, :], unit_raw(c, u), a_hi[:, u % SPLIT, :].bitcast(F32),
                                  ALU.subtract).then_inc(lo_set, 1)

            def blk(t, n, b):
                at = n * COLS + b * P
                return t[:, at:at + P] if isinstance(n, int) else t[:, bass.ds(at, P)]

            def four(t, n):
                return t[:, n * PER:(n + 1) * PER] if isinstance(n, int) else t[:, bass.ds(n * PER, PER)]

            def merge(n, s):
                link = Link(s["chain"], n * MERGE_LINKS)
                dve.wait_ge(s["turned"], n + 1 + s["primed"])
                sums = tiny.rearrange("p (b g k) -> p b g k", b=PER, g=4)[:, :, :, 0:3]
                link(dve.tensor_reduce(four(den_all, n), sums, AX.XY, ALU.add))
                dve.scalar_tensor_tensor(out=four(ok_all, n), in0=four(den_all, n), scalar=LEAST,
                                         in1=four(noneg, n), op0=ALU.is_ge, op1=ALU.mult)
                link(dve.tensor_scalar(small[:, 7, :], four(den_all, n), TINY, None, ALU.max))
                link(dve.reciprocal(small[:, 7, :], small[:, 7, :]))
                link(dve.tensor_tensor(small[:, 7, :], small[:, 7, :], four(ok_all, n), ALU.mult))
                for b in range(PER):
                    old = blk(x_sb, n, b) if s is fast else blk(stage, n, b)
                    ins = dve.scalar_tensor_tensor(out=blk(x_sb, n, b), in0=tp[:, b * P:(b + 1) * P],
                                                   scalar=small[:, 7, b:b + 1], in1=old,
                                                   op0=ALU.mult, op1=ALU.add)
                link(ins, True)
                for b in range(PER):
                    ins = dve.bn_stats(stats[:, b, :], blk(x_sb, n, b))
                link(ins, True)
                for b in range(PER):
                    ins = dve.bn_aggr(mv[:, b, :], stats[:, b, :])
                link(ins)
                dve.tensor_scalar(small[:, 0, :], mv[:, :, 1], EPS, None, ALU.add).then_inc(s["var"], 1)
                assert link.k == 7
                return link

            def renorm(n, s, link):
                root(small, link, s, n)
                for b in range(PER):
                    ins = dve.tensor_scalar(blk(stage, n, b), blk(x_sb, n, b), mv[:, b, 0:1],
                                            small[:, 6, b:b + 1], ALU.subtract, ALU.mult)
                link(ins)
                assert link.k == MERGE_LINKS
                dve.tensor_scalar(stage[:, chunk_cols(n)], stage[:, chunk_cols(n)], 0.0, None, ALU.max)
                dve.tensor_copy(four(var_all, n), small[:, 0, :]).then_inc(s["done"], 1)

            def attention(c, prev):
                for u in range(UNITS):
                    if u % 2 == 0:
                        wait_raw(dve, A_PASS + c, u)
                        wait(dve, unit_used, c * UNITS + u - 2)
                        dve.tensor_scalar(pos[u % SPLIT], unit_raw(c, u), 0.0, None, ALU.is_gt) \
                            .then_inc(pos_even, 1)
                    split_lo(c, A_PASS + c, u)
                    if prev and u == 6:
                        link = merge(c - 1, fast)
                    if prev and u == 9:
                        renorm(c - 1, fast, link)

            dve.wait_ge(hw_done, 16)
            dve.wait_ge(w_set, 1)
            dve.wait_ge(u_lo_set, BLOCKS)
            attention(0, False)
            with dve.Fori(1, CHUNKS) as c:
                attention(c, True)
            renorm(CHUNKS - 1, fast, merge(CHUNKS - 1, fast))

            dve.wait_ge(fast["done"], CHUNKS)
            link(dve.tensor_scalar(var_all[:, :], var_all[:, :], HUGE, None, ALU.is_le))
            link(dve.tensor_tensor(w_all[:, :], ok_all[:, :], var_all[:, :], ALU.mult))
            link(dve.tensor_reduce(bad[:, 0:1], w_all[:, :], AX.X, ALU.min))
            dve.tensor_scalar(bad[:, 1:2], bad[:, 0:1], -1.0, 1.0, ALU.mult, ALU.add).then_inc(bad_set, 1)
            dve.wait_ge(bad_sum, 1)
            dve.tensor_copy(flag[:, :], tiny[:, 0:1]).then_inc(flag_set, 1)

            dve.wait_ge(flag_set, 1)
            with dve.If(dve.value_load(flag[0:1, 0:1], min_val=0, max_val=P) != 0):
                def maxima(c, u, b):
                    m = 2 * c * BLOCKS + u * UB + b
                    j = u * UB + b
                    glink = Link(g_chain, c * G_LINKS + 1 + (u * UB + b) * 5)
                    a = g_a[b]
                    dve.wait_ge(g_landed[b], c * (2 * UNITS * 16) + u * 16 + 16)
                    for k, there, absent in ((0, ALU.is_gt, ALU.is_le), (1, ALU.is_lt, ALU.is_ge)):
                        dve.tensor_scalar(g_t, a, 0.0, e_pm[:, bass.ds(j, 1), k], there, ALU.mult)
                        glink(dve.tensor_scalar(g_s, a, 0.0, -HUGE, absent, ALU.mult))
                        glink(dve.tensor_tensor(g_t, g_t, g_s, ALU.add))
                        ins = dve.tensor_tensor(g_row, g_row, g_t, ALU.max)
                        if k == 0:
                            glink(ins)
                    ins.then_inc(g_freed, 1)
                    dve.wait_ge(g_freed, m + 2)

                def weights(c, u, b):
                    m = (2 * c + 1) * BLOCKS + u * UB + b
                    n = c * BLOCKS + u * UB + b
                    j = u * UB + b
                    glink = Link(g_chain, c * G_LINKS + 2 + BLOCKS * 5 + (u * UB + b) * 3)
                    a = g_a[b]
                    dve.wait_ge(g_landed[b], c * (2 * UNITS * 16) + (UNITS + 1) * 16 + u * 16)
                    dve.tensor_scalar(g_t, g_neg, e_pm[:, bass.ds(j, 1), 0], 0.0, ALU.add, ALU.min).then_inc(g_arg, 1)
                    dve.wait_ge(g_prod, n + 1)
                    dve.wait_ge(g_exp, 2 * n + 1)
                    dve.scalar_tensor_tensor(out=g_num, in0=a, scalar=0.0, in1=g_e, op0=ALU.max, op1=ALU.mult)
                    glink(dve.scalar_tensor_tensor(out=g_den, in0=a, scalar=0.0, in1=g_e,
                                                   op0=ALU.is_gt, op1=ALU.mult))
                    dve.tensor_scalar(g_t, g_neg, e_pm[:, bass.ds(j, 1), 1], 0.0, ALU.add, ALU.min).then_inc(g_arg, 1)
                    dve.wait_ge(g_exp, 2 * n + 2)
                    glink(dve.scalar_tensor_tensor(out=g_s, in0=a, scalar=0.0, in1=g_e, op0=ALU.min, op1=ALU.mult))
                    glink(dve.tensor_tensor(g_num, g_num, g_s, ALU.add))
                    dve.scalar_tensor_tensor(out=g_s, in0=a, scalar=0.0, in1=g_e,
                                             op0=ALU.is_lt, op1=ALU.mult).then_inc(g_freed, 1)
                    dve.wait_ge(g_freed, m + 2)
                    dve.tensor_tensor(g_den, g_den, g_s, ALU.add).then_inc(g_tile, 1)

                for k, s in enumerate((g_freed, g_prod, slow["turned"], slow["done"])):
                    dve.memset(gate[:, k + 2:k + 3], 0.0).then_inc(s, 1)
                dve.memset(noneg[:, :], 1.0).then_inc(g_noneg, 1)
                dve.wait_ge(g_noneg, 1)
                dve.wait_ge(g_x, 16)
                with dve.Fori(0, CHUNKS) as c:
                    glink = Link(g_chain, c * G_LINKS)
                    glink(dve.memset(g_row, -HUGE), True)
                    with dve.Fori(0, UNITS) as u:
                        for b in range(UB):
                            maxima(c, u, b)
                    dve.wait_ge(g_all, c + 1)
                    dve.tensor_scalar(g_neg, g_e, -1.0, None, ALU.mult).then_inc(g_chain, 1)
                    dve.wait_ge(g_chain, c * G_LINKS + 2 + BLOCKS * 5)
                    dve.memset(gate[:, 0:1], 0.0)
                    with dve.Fori(0, UNITS) as u:
                        for b in range(UB):
                            weights(c, u, b)
                    renorm(c, slow, merge(c, slow))
                    dve.wait_ge(slow["done"], c + 2)

            def fill_lo(n):
                s = n
                cols = slice(s * COLS, (s + 1) * COLS)
                dve.tensor_tensor(u_lo[:, cols], stage[:, cols], u_hi[:, cols].bitcast(F32), ALU.subtract) \
                    .then_inc(u_lo_set, 1)

            def leaky(h, ready, m, done):
                dve.wait_ge(ready, m + 1)
                dve.scalar_tensor_tensor(out=h[:, :], in0=h[:, :], scalar=SLOPE, in1=h[:, :],
                                         op0=ALU.mult, op1=ALU.max).then_inc(done, 1)

            def features(m, c, mlp):
                dve.wait_ge(z3_set, m + 1)
                dve.tensor_tensor(h1[:, :].rearrange("p (b f) -> p b f", b=PER),
                                  tp.rearrange("p (b f) -> p b f", b=PER), mlp.b3, ALU.add).then_inc(t3_set, 1)
                dve.wait_ge(t3_set, m + 1)
                dve.scalar_tensor_tensor(out=stage[:, chunk_cols(c)], in0=h1[:, :], scalar=SLOPE, in1=h1[:, :],
                                         op0=ALU.mult, op1=ALU.max).then_inc(fresh, 1)

            def passing(m, c, mlp, prev, start, r, prev_c):
                def fill(s):
                    dve.wait_ge(u_hi_set, BLOCKS + r * CHUNKS + s + 1)
                    fill_lo(s)

                for u in range(UNITS):
                    split_lo(c, M_PASS + m, u)
                    if start and u == 2:
                        fill(0)
                        fill(1)
                    if start and 3 <= u <= 7:
                        fill(u - 1)
                    if prev and u == 5:
                        leaky(h1, bias1_set, m - 1, h1_set)
                    if prev and u == 8:
                        leaky(h2, bias2_set, m - 1, h2_set)
                    if prev and u == 11:
                        features(m - 1, prev_c, mlp)
                    if start and u == 12:
                        fill(7)

            def a_round(r, mlp, prev_mlp):
                m = r * CHUNKS
                passing(m, 0, prev_mlp, prev_mlp is not None, True, r, CHUNKS - 1)
                with dve.Fori(1, CHUNKS) as c:
                    passing(m + c, c, mlp, True, False, r, c - 1)

            a_round(0, uv, None)
            with dve.Fori(0, (ROUNDS - 1) // 2) as q:
                a_round(2 * q + 1, vu, uv)
                a_round(2 * q + 2, uv, vu)
            m = ROUNDS * CHUNKS - 1
            leaky(h1, bias1_set, m, h1_set)
            leaky(h2, bias2_set, m, h2_set)
            features(m, CHUNKS - 1, uv)
            for c in range(CHUNKS):
                cols = slice(c * COLS, (c + 1) * COLS)
                dve.wait_ge(fresh, (ROUNDS - 1) * CHUNKS + c + 1)
                dve.tensor_tensor(stage[:, cols], stage[:, cols], x_sb[:, cols], ALU.add).then_inc(final, 1)

        @block.tensor
        def _(pe):
            pe.wait_ge(params_in_sb, 16)
            pe.wait_ge(pick_set, 1)
            w0 = params[:, W0:W0 + P]
            def project(c):
                pe.wait_ge(first["done"], c + 1)
                wait(pe, pre_y, c)
                for b in range(PER):
                    mm = pe.transpose(tp[:, b * P:(b + 1) * P], h2[:, b * P:(b + 1) * P], ident)
                mm.then_inc(pre_t, 1)
                pe.wait_ge(pre_y, c + 1)
                wait(pe, pre_h1, c)
                pe.matmul(z1, w0, y[:, :], start=True, stop=True).then_inc(pre_hwt, 1)
                wait(pe, pre_st, c)
                for b in range(PER):
                    mm = pe.matmul(z2[:, b * P:(b + 1) * P], y[:, b * P:(b + 1) * P], w0, start=True, stop=True)
                mm.then_inc(pre_hw, 1)
                pe.wait_ge(pre_h1, c + 1)
                wait(pe, pre_pc, c)
                for b in range(PER):
                    mm = pe.matmul(tiny[:, 2 * b:2 * b + 2], h1[:, b * P:(b + 1) * P], a12, start=True, stop=True)
                mm.then_inc(pre_p, 1)

            project(0)
            with pe.Fori(1, CHUNKS) as c:
                project(c)

            def e_turn(c):
                pe.wait_ge(params_in_sb, 16)
                pe.wait_ge(e_row, c + 1)
                wait(pe, e_col, c)
                for b in range(PER):
                    mm = pe.transpose(tiny[:, 8 * b:8 * b + 7], y[0:7, b * P:(b + 1) * P], ident[0:7, 0:7])
                mm.then_inc(e_turned, 1)

            def e_chunk(c, par, prev):
                wait(pe, e_row, c - 1)
                for u in range(UNITS):
                    pe.wait_ge(masked, c * UNITS + u + 1)
                    for b in range(UB):
                        j = u * UB + b
                        for g in range(2):
                            mm = pe.matmul(row[par][0:7, :], probe[:, j, 7 * g:7 * g + 7],
                                           masks[:, u % SPLIT, g, b * COLS:(b + 1) * COLS],
                                           start=(j == 0 and g == 0), stop=(j == BLOCKS - 1 and g == 1))
                    mm.then_inc(mask_used, 1)
                    if prev and u == 3:
                        e_turn(c - 1)

            pe.wait_ge(probe_set, 1)
            for par in range(2):
                e_chunk(par, par, par == 1)
            with pe.Fori(1, CHUNKS // 2) as k:
                for par in range(2):
                    e_chunk(2 * k + par, par, True)
            e_turn(CHUNKS - 1)

            def products(m_abs, par, u, stationary_ready, sums):
                v = m_abs * UNITS + u
                pe.wait_ge(hi_set, v + 1)
                pe.wait_ge(lo_set, v + 1)
                if sums and u % 2:
                    pe.wait_ge(pos_even, m_abs * (UNITS // 2) + u // 2 + 1)
                    pe.wait_ge(pos_odd, m_abs * (UNITS // 2) + u // 2 + 1)
                    for g in range(2 * UB):
                        j = (u - 1) * UB + g
                        pe.matmul(psum[32 * g:32 * g + 32, 2 + par, :], wpart[:, j, :],
                                  pos[(j // UB) % SPLIT][:, (j % UB) * COLS:(j % UB + 1) * COLS],
                                  start=(u == 1), stop=(u == UNITS - 1), tile_position=(0, 32 * g))
                for b in range(UB):
                    j = u * UB + b
                    stationary_ready(j)
                    cols, mov = slice(j * P, (j + 1) * P), slice(b * COLS, (b + 1) * COLS)
                    hi, lo = a_hi[:, u % SPLIT, mov], a_lo[:, u % SPLIT, mov]
                    pe.matmul(acc[par], u_hi[:, cols], hi, start=(j == 0), stop=False)
                    pe.matmul(acc[par], u_hi[:, cols], lo, start=False, stop=False)
                    mm = pe.matmul(acc[par], u_lo[:, cols], hi, start=False, stop=(j == BLOCKS - 1))
                mm.then_inc(unit_used, 1)

            def turn(n, s):
                pe.wait_ge(s["copied"], n + 1)
                wait(pe, s["done"], n + s["primed"])
                for b in range(PER):
                    pe.transpose(tp[:, b * P:(b + 1) * P], y[:, b * P:(b + 1) * P], ident)
                for b in range(PER):
                    mm = pe.transpose(tiny[:, b * P:(b + 1) * P], h2[:, b * P:(b + 1) * P], ident)
                mm.then_inc(s["turned"], 1)

            def attention(c, par, prev):
                wait(pe, fast["copied"], c - 1)
                for u in range(UNITS):
                    def ready(j):
                        if isinstance(c, int) and c == 0:
                            pe.wait_ge(u_lo_set, j + 1)
                    products(c, par, u, ready, True)
                    if prev and u == 5:
                        turn(c - 1, fast)

            pe.wait_ge(w_set, 1)
            attention(0, 0, False)
            attention(1, 1, True)
            with pe.Fori(1, CHUNKS // 2) as k:
                for par in range(2):
                    attention(2 * k + par, par, True)
            turn(CHUNKS - 1, fast)

            pe.wait_ge(bad_set, 1)
            pe.matmul(tiny[:, 0:1], pick[:, :], bad[:, 1:2], start=True, stop=True).then_inc(bad_sum, 1)
            pe.wait_ge(flag_set, 1)
            with pe.If(pe.value_load(flag[0:1, 0:1], min_val=0, max_val=P) != 0):
                def tile(c, u, b, begin, end):
                    n = c * BLOCKS + u * UB + b
                    pe.wait_ge(hw_landed[b], c * (UNITS * 16) + u * 16 + 16)
                    pe.wait_ge(g_tile, n + 1)
                    pe.matmul(acc[0], g_hw[b], g_num, start=begin, stop=end)
                    pe.matmul(row[0], pick[:, :], g_den, start=begin, stop=end).then_inc(g_prod, 1)

                with pe.Fori(0, CHUNKS) as c:
                    tile(c, 0, 0, True, False)
                    tile(c, 0, 1, False, False)
                    with pe.Fori(1, UNITS - 1) as u:
                        tile(c, u, 0, False, False)
                        tile(c, u, 1, False, False)
                    tile(c, UNITS - 1, 0, False, False)
                    tile(c, UNITS - 1, 1, False, True)
                    turn(c, slow)

            def mlp1(m, mlp):
                pe.wait_ge(y_set, m + 1)
                wait(pe, bias1_set, m)
                pe.matmul(z1, mlp.w[0], y[:, :], start=True, stop=True).then_inc(z1_set, 1)

            def mlp2(m, mlp):
                pe.wait_ge(h1_set, m + 1)
                wait(pe, bias2_set, m)
                pe.matmul(z2, mlp.w[1], h1[:, :], start=True, stop=True).then_inc(z2_set, 1)

            def mlp3(m, mlp):
                pe.wait_ge(h2_set, m + 1)
                wait(pe, t3_set, m)
                for b in range(PER):
                    mm = pe.matmul(tp[:, b * P:(b + 1) * P], h2[:, b * P:(b + 1) * P], mlp.w[2],
                                   start=True, stop=True)
                mm.then_inc(z3_set, 1)

            def passing(m, par, mlp, prev, start, r):
                wait(pe, y_set, m - 1)
                for u in range(UNITS):
                    def ready(j):
                        if start and j % PER == 0:
                            pe.wait_ge(u_lo_set, BLOCKS + r * CHUNKS + j // PER + 1)
                    products(CHUNKS + m, par, u, ready, False)
                    if prev and u == 1:
                        mlp1(m - 1, mlp)
                    if prev and u == 4:
                        mlp2(m - 1, mlp)
                    if prev and u == 7:
                        mlp3(m - 1, mlp)

            def a_round(r, mlp, prev_mlp):
                m = r * CHUNKS
                passing(m, 0, prev_mlp, prev_mlp is not None, True, r)
                passing(m + 1, 1, mlp, True, False, r)
                with pe.Fori(1, CHUNKS // 2) as k:
                    for par in range(2):
                        passing(m + 2 * k + par, par, mlp, True, False, r)

            a_round(0, uv, None)
            with pe.Fori(0, (ROUNDS - 1) // 2) as q:
                a_round(2 * q + 1, vu, uv)
                a_round(2 * q + 2, uv, vu)
            m = ROUNDS * CHUNKS - 1
            mlp1(m, uv)
            mlp2(m, uv)
            mlp3(m, uv)


def kernel(x, adj, L0_gnn_W, L0_gnn_a, L1_gnn_v_node_feats, L1_gnn_uv_W1, L1_gnn_uv_b1, L1_gnn_uv_W2,
           L1_gnn_uv_b2, L1_gnn_uv_W3, L1_gnn_uv_b3, L1_gnn_vu_W1, L1_gnn_vu_b1, L1_gnn_vu_W2,
           L1_gnn_vu_b2, L1_gnn_vu_W3, L1_gnn_vu_b3):
    import numpy as np
    import concourse.bacc as bacc
    from concourse.bass_utils import run_bass_kernel_spmd

    a = np.asarray(adj).reshape(P, CHUNKS, PER, P, UNITS, UB).transpose(1, 4, 3, 5, 2, 0)
    a = np.ascontiguousarray(a).reshape(CHUNKS * UNITS, P, UW)
    rows = [np.broadcast_to(np.asarray(b)[None, :], (P, P)) for b in (L1_gnn_uv_b3, L1_gnn_vu_b3)]
    columns = [np.asarray(b)[:, None] for b in (L1_gnn_uv_b1, L1_gnn_uv_b2, L1_gnn_vu_b1, L1_gnn_vu_b2)]
    halves = np.asarray(L0_gnn_a).reshape(2, P).transpose()
    params = np.concatenate(
        [np.asarray(w) for w in (L0_gnn_W, L1_gnn_uv_W1, L1_gnn_uv_W2, L1_gnn_uv_W3, L1_gnn_vu_W1,
                                 L1_gnn_vu_W2, L1_gnn_vu_W3)]
        + rows + [np.eye(P, dtype=np.float32), halves] + columns, axis=1)
    arrays = {"x_in": np.ascontiguousarray(np.asarray(x)).reshape(P, N), "adj_in": a,
              "params_in": np.ascontiguousarray(params)}

    nc = bacc.Bacc("TRN2", target_bir_lowering=False, num_devices=1)
    ins = {k: nc.dram_tensor(k, v.shape, F32, kind="ExternalInput").ap() for k, v in arrays.items()}
    out = nc.dram_tensor("out", (P, N), F32, kind="ExternalOutput").ap()
    hw_dram = nc.dram_tensor("hw_dram", (P, N), F32, kind="Internal").ap()
    build(nc, ins["x_in"], ins["adj_in"], ins["params_in"], out, hw_dram)
    got = run_bass_kernel_spmd(nc, [arrays], core_ids=[0])
    return np.asarray(got.results[0]["out"]).reshape(N, P)
```

```python
from contextlib import ExitStack

import concourse.bass as bass
from concourse import mybir

P = 128
N = 4096
BLOCKS = N // P
COLS = 512
CHUNKS = N // COLS
PER = COLS // P
UB = 2
UNITS = BLOCKS // UB
UW = UB * COLS
KEPT = 2
RING = 7
STREAMED = UNITS - KEPT
LAPS = STREAMED // RING
SPLIT = 4
DIRECT = (6, 8, 10, 12)
SPLITS = UNITS - len(DIRECT)
LO_FILLS = BLOCKS - UB * len(DIRECT)
ROUNDS = 5
EPS = 1e-5
SLOPE = 0.01
E_SLOPE = 0.2
TOP = 75.0
LEAST = 1e-24
HUGE = 3.0e38
TINY = 1e-37

F32 = mybir.dt.float32
F32R = mybir.dt.float32r
BF16 = mybir.dt.bfloat16
I32 = mybir.dt.int32
ALU = mybir.AluOpType
ACT = mybir.ActivationFunctionType
AX = mybir.AxisListType
RMAX = bass.bass_isa.ReduceOp.max

UV, VU, B3UV, B3VU, IDENT, A12, BIAS, W0 = 0, 384, 768, 896, 1024, 1152, 1154, 1158
PARAMS = W0 + P
G_LINKS = 2 + BLOCKS * (5 + 3)
ROOT_LINKS = 5
MERGE_LINKS = 4 + 1 + 2 + ROOT_LINKS


def build(nc, x_in, adj, params_in, out, hw_dram):
    assert STREAMED % RING == 0 and UNITS % SPLIT == 0
    ctx = ExitStack()
    with ctx:
        def sb(name, shape, dt):
            return ctx.enter_context(nc.sbuf_tensor(name, shape, dt))

        def sem(name):
            return ctx.enter_context(nc.semaphore(name))

        params = sb("params", [P, PARAMS + 2], F32)
        x_sb = sb("x_sb", [P, N], F32)
        stage = sb("stage", [P, N], F32)
        u_hi = sb("u_hi", [P, N], F32R)
        scratch_at = nc.sbuf_base
        u_lo = sb("u_lo", [P, N], F32R)
        scratch = nc.alloc_sbuf_tensor_at("scratch", [P, N], F32, offset=scratch_at)
        kept = sb("kept", [P, CHUNKS, KEPT * UW], F32)
        ring = sb("ring", [P, RING, UW], F32)
        a_hi = sb("a_hi", [P, SPLIT, UW], F32R)
        early_at = nc.sbuf_base + KEPT * UW * 4
        a_lo = sb("a_lo", [P, SPLIT, UW], F32R)
        probe = nc.alloc_sbuf_tensor_at("probe", [P, BLOCKS, 14], BF16, offset=early_at)
        early = nc.alloc_sbuf_tensor_at("early", [P, 26 * BLOCKS], F32, offset=early_at + 28 * BLOCKS)
        pos2_at = nc.sbuf_base
        pos2 = sb("pos2", [P, 2, UW], BF16)
        w_hi = nc.alloc_sbuf_tensor_at("w_hi", [P, 2, 2 * P], F32R, offset=pos2_at)
        w_lo = nc.alloc_sbuf_tensor_at("w_lo", [P, 2, 2 * P], F32R, offset=pos2_at + 16 * P)
        y_at = nc.sbuf_base
        y = sb("y", [P, COLS], F32)
        in_hi = nc.alloc_sbuf_tensor_at("in_hi", [P, COLS], F32R, offset=y_at)
        h1 = sb("h1", [P, COLS], F32)
        h2 = sb("h2", [P, COLS], F32)
        wpart_at = nc.sbuf_base
        wpart = sb("wpart", [P, BLOCKS, 32], BF16)
        in_lo = nc.alloc_sbuf_tensor_at("in_lo", [P, COLS], F32R, offset=wpart_at)
        e_pm = sb("e_pm", [P, BLOCKS, 2], F32)
        w_all = sb("w_all", [P, BLOCKS], F32)
        den_all = sb("den_all", [P, BLOCKS], F32)
        var_all = sb("var_all", [P, BLOCKS], F32)
        good = sb("good", [P, 1], F32)
        flag = sb("flag", [P, 1], I32)
        top = sb("top", [P, 2], F32)
        stats = sb("stats", [P, PER, 6], F32)
        mv = sb("mv", [P, PER, 2], F32)
        small = sb("small", [P, 8, PER], F32)
        ok_all = sb("ok_all", [P, BLOCKS], F32)
        noneg = sb("noneg", [P, BLOCKS], F32)
        gate = sb("gate", [P, 6], F32)
        pick = sb("pick", [P, P], F32)
        psum = ctx.enter_context(nc.psum_tensor("psum", [P, 8, COLS], F32))
        acc = [psum[:, 0, :], psum[:, 1, :]]
        row = [psum[:, 2, :], psum[:, 3, :]]
        z1, z2, tp, tiny = (psum[:, k, :] for k in (4, 5, 6, 7))

        pos = [pos2[:, 0, :], pos2[:, 1, :], stage[:, N - COLS:].bitcast(BF16), h1[:, :].bitcast(BF16)]
        norm2 = [h2[:, :], pos2[:, 0, :].bitcast(F32)]
        turned2, hwt2 = [tp, tiny], [y[:, :], h1[:, :]]
        hwp2 = [psum[:, k:k + 2, 0:2 * (P + 2)].rearrange("p k (b f) -> p k b f", b=2) for k in (2, 4)]
        ident = params[:, IDENT:IDENT + P]
        a12 = params[:, A12:A12 + 2]
        masks = scratch[:, :].bitcast(BF16).rearrange("p (s g c) -> p s g c", s=SPLIT, g=2)
        fb = scratch[:, :].rearrange("p (k c) -> p k c", c=COLS)
        g_a = [fb[:, 0, :], fb[:, 1, :]]
        g_row, g_neg, g_t, g_e, g_num, g_den = (fb[:, k, :] for k in range(2, 8))
        g_s = h1[:, :]
        g_hw = [h2[:, 0:P], h2[:, P:2 * P]]
        e_plus, e_minus = e_pm[:, :, 0], e_pm[:, :, 1]

        def early_part(at, k):
            return early[:, at * BLOCKS:(at + k) * BLOCKS].rearrange("p (b k) -> p b k", k=k)

        stats0, mv0 = early_part(0, 6), early_part(6, 2)
        root0 = early[:, 8 * BLOCKS:15 * BLOCKS].rearrange("p (k b) -> p k b", k=7)
        p_all = early_part(15, 2)
        rest = early_part(17, 2)
        e_all = early_part(19, 7)
        e_sum = early_part(0, 2)

        class Mlp:
            def __init__(self, at, b3, b, k):
                self.hi = [w_hi[:, k, i * P:(i + 1) * P] for i in range(2)]
                self.lo = [w_lo[:, k, i * P:(i + 1) * P] for i in range(2)]
                self.w = [params[:, at + k * P:at + (k + 1) * P] for k in range(3)]
                self.b1, self.b2 = params[:, BIAS + b:BIAS + b + 1], params[:, BIAS + b + 1:BIAS + b + 2]
                self.b3 = params[:, b3:b3 + P].unsqueeze(1).broadcast_to([P, PER, P])

        HALVES = 2
        half_cols = [slice(h * COLS // HALVES, (h + 1) * COLS // HALVES) for h in range(HALVES)]
        end_z1, end_z2, end_z3 = ([bank[:, half_cols[0]] for bank in pair]
                                  for pair in ((z1, row[0]), (z2, row[1]), (tp, tiny)))

        uv, vu = Mlp(UV, B3UV, 0, 0), Mlp(VU, B3VU, 2, 1)
        both_w12 = params[:, UV:UV + 6 * P].rearrange("p (k w) -> p k w", k=2)[:, :, 0:2 * P]

        params_in_sb, kept_in = sem("params_in_sb"), sem("kept_in")
        x_in_sb = [sem(f"x_in_sb{q}") for q in range(4)]
        landed = [sem(f"landed{s}") for s in range(RING)]
        hw_done, hw_end_done, out_done = sem("hw_done"), sem("hw_end_done"), sem("out_done")
        pick_set = sem("pick_set")

        def norm_sems(tag):
            return {k: sem(f"{tag}_{k}") for k in ("chain", "var", "std", "done")}

        first = norm_sems("first")
        pre_t, pre_y, pre_hw, pre_st, pre_pc = (
            sem(f"pre_{k}") for k in ("turned", "y", "hw", "stage", "pcopied"))
        w0_turned, w0_copied, w0a_summed, w0a_set = (
            sem(k) for k in ("w0_turned", "w0_copied", "w0a_summed", "w0a_set"))
        masked, mask_used = sem("masked"), sem("mask_used")
        e_row, e_turned, e_col = sem("e_row"), sem("e_turned"), sem("e_col")
        chain = sem("chain")
        probe_set, top_part, top_all, shifted, w_exp, w_set = (
            sem(k) for k in ("probe_set", "top_part", "top_all", "shifted", "w_exp", "w_set"))
        u_hi_set, u_lo_set = sem("u_hi_set"), sem("u_lo_set")
        hi_set, lo_set, unit_used = sem("hi_set"), sem("lo_set"), sem("unit_used")
        pos_by_dve, pos_by_act = sem("pos_by_dve"), sem("pos_by_act")
        w_hi_set, w_lo_set, y_lo_set, h1_hi_set, h1_lo_set = (
            sem(k) for k in ("w_hi_set", "w_lo_set", "y_lo_set", "h1_hi_set", "h1_lo_set"))
        bias1_set, bias2_set = sem("bias1_set"), sem("bias2_set")
        y_set, z1_set, h1_set, z2_set, h2_set, z3_set, t3_set, fresh = (
            sem(k) for k in ("y_set", "z1_set", "h1_set", "z2_set", "h2_set", "z3_set", "t3_set", "fresh"))

        def merge_sems(tag):
            got = norm_sems(tag)
            got.update({k: sem(f"{tag}_{k}") for k in ("copied", "turned")})
            got["primed"] = int(tag == "slow")
            return got

        fast, slow = merge_sems("fast"), merge_sems("slow")
        good_set, good_sum, flag_set = sem("good_set"), sem("good_sum"), sem("flag_set")
        final = sem("final")
        g_landed = [sem("g_landed0"), sem("g_landed1")]
        hw_landed = [sem("hw_landed0"), sem("hw_landed1")]
        g_noneg = sem("g_noneg")
        g_x, g_freed, g_chain, g_all, g_arg, g_exp, g_tile, g_prod = (
            sem(f"g_{k}") for k in ("x", "freed", "chain", "all", "arg", "exp", "tile", "prod"))

        block = ctx.enter_context(nc.Block())

        def wait(eng, s, value):
            if not isinstance(value, int) or value > 0:
                eng.wait_ge(s, value)

        class Link:

            def __init__(self, s, base=0):
                self.s, self.base, self.k = s, base, 0

            def __call__(self, ins, gated=False):
                self.k += 1
                ins.then_inc(self.s, 1)
                nc.vector.wait_ge(self.s, self.base + self.k)
                if gated:
                    nc.vector.memset(gate[:, 0:1], 0.0)

        def chunk_cols(c):
            return bass.ds(c * COLS, COLS) if not isinstance(c, int) else slice(c * COLS, (c + 1) * COLS)

        def unit_raw(c, u):
            return kept[:, c, u * UW:(u + 1) * UW] if u < KEPT else ring[:, (u - KEPT) % RING, :]

        def wait_raw(eng, t, u):
            if u >= KEPT:
                n = u - KEPT
                eng.wait_ge(landed[n % RING], 16 * (LAPS * t + n // RING + 1))

        act_masks = {u for u in range(UNITS) if u % 2 or u in (6, 12)}

        def masks_made(by_act, m, u):
            return m * (len(act_masks) if by_act else UNITS - len(act_masks)) \
                + sum((v in act_masks) == by_act for v in range(u + 1))

        def split_no(u):
            return sum(v not in DIRECT for v in range(u))

        fills = [0, 1, 2, 3, 28, 29, 4, 5, 30, 31] + list(range(6, 28))

        def fills_of(r):
            if isinstance(r, int) and r == 0:
                return {u: (0, u) for u in range(CHUNKS)}
            return {u: (r, s) for u, s in ((1, 4), (4, 5), (7, 6), (AT_UNSPLIT["features"] + 1, 7))}

        def fills_ahead(r):
            return {u: (r, s) for u, s in ((5, 0), (8, 1), (11, 2), (14, 3))}

        lo_fills = [b for b in fills if b // UB not in DIRECT]

        def fills_at(u):
            return fills[0:2] if u == 0 else fills[4 * u - 2:4 * u + 2] if u < 3 else fills[4 + 2 * u:6 + 2 * u]

        AT = {"y_copy": 2, "y_lo": 2, "mlp1": 1, "bias1": 5, "leaky1": 5, "h1_hi": 6, "h1_lo": 6,
              "mlp2": 5, "bias2": 9, "leaky2": 9, "mlp3": 8, "features": 12}
        AT_UNSPLIT = {"y_copy": 2, "mlp1": 1, "bias1": 5, "leaky1": 5, "mlp2": 4, "bias2": 8, "leaky2": 8,
                      "mlp3": 7, "features": 11}

        AHEAD_LO = SPLIT - 1
        split_mlps = CHUNKS - 2

        def is_split(c):
            return not isinstance(c, int) or 1 <= c <= split_mlps

        def split_mlp_no(r, c):
            return r * split_mlps + c

        A_PASS, M_PASS = CHUNKS, 2 * CHUNKS

        @block.sync
        def _(sp):
            def load(c, u, n):
                sp.dma_start(ring[:, n % RING, :], adj[c * UNITS + u]).then_inc(landed[n % RING], 16)

            for q in range(4):
                sp.dma_start(x_sb[:, q * 1024:(q + 1) * 1024],
                             x_in[:, q * 1024:(q + 1) * 1024]).then_inc(x_in_sb[q], 16)
            sp.dma_start(params[:, 0:PARAMS], params_in).then_inc(params_in_sb, 16)
            for c in range(CHUNKS):
                for k in range(KEPT):
                    sp.dma_start(kept[:, c, k * UW:(k + 1) * UW], adj[c * UNITS + k]).then_inc(kept_in, 16)

            def first_pass(c):
                for n in range(STREAMED):
                    wait(sp, masked, c * UNITS + n + KEPT - RING + 1 if n >= RING
                         else (c - 1) * UNITS + n + KEPT + RING + 1)
                    load(c, n + KEPT, n)

            def attention_done(c, u):
                if u in DIRECT:
                    by_act = u in act_masks
                    sp.wait_ge(unit_used, c * UNITS + u + 1)
                    sp.wait_ge(pos_by_act if by_act else pos_by_dve, masks_made(by_act, c, u))
                else:
                    sp.wait_ge(hi_set, c * SPLITS + split_no(u) + 1)
                    sp.wait_ge(lo_set, c * SPLITS + split_no(u) + 1)

            def attention_load(c, n):
                if n >= RING:
                    attention_done(c, n + KEPT - RING)
                elif isinstance(c, int) and c == 0:
                    sp.wait_ge(masked, CHUNKS * UNITS)
                else:
                    attention_done(c - 1, n + KEPT + RING)
                load(c, n + KEPT, n)

            def round_load(m, c, n):
                if n < RING and isinstance(m, int) and m == 0:
                    attention_done(CHUNKS - 1, n + KEPT + RING)
                else:
                    v = CHUNKS * SPLITS + (m * UNITS + n + KEPT - RING if n >= RING
                                           else (m - 1) * UNITS + n + KEPT + RING) + 1
                    sp.wait_ge(hi_set, v)
                    sp.wait_ge(lo_set, v)
                load(c, n + KEPT, n)

            first_pass(0)
            with sp.Fori(1, CHUNKS) as c:
                first_pass(c)
            for n in range(STREAMED):
                attention_load(0, n)
            with sp.Fori(1, CHUNKS) as c:
                for n in range(STREAMED):
                    attention_load(c, n)
            for n in range(RING):
                round_load(0, 0, n)

            sp.wait_ge(flag_set, 1)
            sp.wait_ge(hw_done, 16)
            sp.wait_ge(hw_end_done, 16)
            with sp.If(sp.value_load(flag[0:1, 0:1], min_val=0, max_val=P) != 0):
                sp.wait_ge(fast["done"], CHUNKS)
                sp.dma_start(stage[:, :], x_in).then_inc(g_x, 16)
                with sp.Fori(0, CHUNKS) as c:
                    for phase in range(2):
                        with sp.Fori(0, UNITS) as u:
                            for b in range(UB):
                                m = (c * 2 + phase) * BLOCKS + u * UB
                                sp.wait_ge(g_freed, m + 1)
                                if phase:
                                    sp.wait_ge(g_prod, c * BLOCKS + u * UB + 1)
                                    sp.dma_start(g_hw[b], hw_dram[:, bass.ds(u * (UB * P) + b * P, P)]) \
                                        .then_inc(hw_landed[b], 16)
                                sp.dma_start(g_a[b], adj[c * UNITS + u][:, b * COLS:(b + 1) * COLS]) \
                                    .then_inc(g_landed[b], 16)

            for n in range(RING, STREAMED):
                round_load(0, 0, n)
            with sp.Fori(1, CHUNKS) as c:
                for n in range(STREAMED):
                    round_load(c, c, n)
            with sp.Fori(1, ROUNDS) as r:
                with sp.Fori(0, CHUNKS) as c:
                    for n in range(STREAMED):
                        round_load(r * CHUNKS + c, c, n)
            pieces = [(c * COLS, (c + 1) * COLS) for c in range(CHUNKS - 1)]
            pieces += [(N - COLS + cols.start, N - COLS + cols.stop) for cols in half_cols]
            for k, (begin, end) in enumerate(pieces):
                sp.wait_ge(final, k + 1)
                sp.dma_start(out[:, begin:end], stage[:, begin:end]).then_inc(out_done, 16)
            sp.wait_ge(out_done, 16 * len(pieces))

        @block.gpsimd
        def _(pool):
            nc.gpsimd.memset(pick[:, 0:1], 1.0)
            nc.gpsimd.memset(pick[:, 1:P], 0.0).then_inc(pick_set, 1)
            pool.wait_ge(top_part, 1)
            nc.gpsimd.partition_all_reduce(top[:, 1:2], top[:, 0:1], P, RMAX).then_inc(top_all, 1)
            pool.wait_ge(flag_set, 1)
            with pool.If(pool.value_load(flag[0:1, 0:1], min_val=0, max_val=P) != 0):
                with pool.Fori(0, CHUNKS) as c:
                    pool.wait_ge(g_freed, (2 * c + 1) * BLOCKS + 1)
                    nc.gpsimd.tensor_tensor(gate[:, 1:2], pick[:, 0:1], pick[:, 1:2], ALU.mult)
                    nc.gpsimd.partition_all_reduce(g_e, g_row, P, RMAX).then_inc(g_all, 1)

        @block.scalar
        def _(act):
            act.wait_ge(w0_turned, 1)
            act.activation(stage[:, 0:P], acc[0][:, 0:P], ACT.Copy).then_inc(w0_copied, 1)
            act.wait_ge(w0a_summed, 1)
            act.activation(params[:, PARAMS:PARAMS + 2], acc[1][:, 0:2], ACT.Copy).then_inc(w0a_set, 1)
            act.wait_ge(first["var"], 1)
            act.activation(root0[:, 1, :], root0[:, 0, :], ACT.Sqrt).then_inc(first["std"], 1)

            def relu(c, par):
                act.wait_ge(pre_t, c + 1)
                wait(act, pre_hw, c - 1)
                act.activation(hwt2[par], turned2[par], ACT.Relu).then_inc(pre_y, 1)

            def keep_hw(c, par):
                act.wait_ge(pre_hw, c + 1)
                act.activation(stage[:, chunk_cols(c)].rearrange("p (k b f) -> p k b f", k=2, b=2),
                               hwp2[par][:, :, :, 0:P], ACT.Copy).then_inc(pre_st, 1)

            relu(0, 0)
            relu(1, 1)
            keep_hw(0, 0)
            with act.Fori(1, CHUNKS // 2) as k:
                for par in range(2):
                    relu(2 * k + par, par)
                    keep_hw(2 * k + par - 1, 1 - par)
            keep_hw(CHUNKS - 1, 1)

            act.wait_ge(pre_st, CHUNKS)
            act.dma_start(hw_dram[:, N - COLS:], stage[:, N - COLS:]).then_inc(hw_end_done, 16)

            def e_copy(c, par):
                act.wait_ge(mask_used, (c + 1) * UNITS)
                wait(act, e_turned, c)
                act.activation(y[0:7, :], row[par][0:7, :], ACT.Copy).then_inc(e_row, 1)

            def split_hi(c, t, u, free):
                wait_raw(act, t, u)
                wait(act, unit_used, free)
                act.activation(a_hi[:, u % SPLIT, :], unit_raw(c, u), ACT.Copy).then_inc(hi_set, 1)

            def pos_mask(c, u):
                act.activation(pos[u % SPLIT], unit_raw(c, u), ACT.Sign).then_inc(pos_by_act, 1)

            act.wait_ge(kept_in, 16 * CHUNKS * KEPT)
            for u in range(KEPT):
                split_hi(0, A_PASS, u, 0)
                if u in act_masks:
                    pos_mask(0, u)

            e_copy(0, 0)
            e_copy(1, 1)
            with act.Fori(1, CHUNKS // 2) as k:
                for par in range(2):
                    e_copy(2 * k + par, par)

            act.wait_ge(shifted, 1)
            act.activation(w_all[:, :], e_sum[:, :, 0], ACT.Exp).then_inc(w_exp, 1)
            act.wait_ge(pre_st, CHUNKS)
            act.dma_start(hw_dram[:, 0:N - COLS], stage[:, 0:N - COLS]).then_inc(hw_done, 16)
            act.wait_ge(w_exp, 1)

            def weight_hi(b):
                to = scratch[:, b * P:(b + 1) * P] if b // UB in DIRECT else u_hi[:, b * P:(b + 1) * P]
                act.activation(to, stage[:, b * P:(b + 1) * P], ACT.Copy,
                               scale=w_all[:, b:b + 1]).then_inc(u_hi_set, 1)

            def merge_copy(n, s, num, den):
                if s is fast:
                    act.wait_ge(unit_used, (n + 1) * UNITS)
                else:
                    act.wait_ge(g_prod, (n + 1) * BLOCKS + 1)
                wait(act, s["turned"], n + s["primed"])
                act.activation(y[:, :], num, ACT.Copy)
                act.activation(h2[:, :], den, ACT.Copy).then_inc(s["copied"], 1)

            def merge_root(n, s):
                act.wait_ge(s["var"], n + 1)
                act.activation(small[:, 1, :], small[:, 0, :], ACT.Sqrt).then_inc(s["std"], 1)

            def attention(c, par, prev):
                for u in range(UNITS):
                    if not prev:
                        for b in fills_at(u):
                            weight_hi(b)

                    if u in act_masks and u >= KEPT:
                        wait_raw(act, A_PASS + c, u)
                        wait(act, unit_used, c * UNITS + u - SPLIT + 1 + (u + 1) % 2)
                        pos_mask(c, u)
                    if u not in DIRECT and (prev or u >= KEPT):
                        split_hi(c, A_PASS + c, u, c * UNITS + u - SPLIT + 1)
                    if u in act_masks and u < KEPT and prev:
                        pos_mask(c, u)
                    if prev and u == 3:
                        merge_copy(c - 1, fast, acc[1 - par], row[1 - par])
                    if prev and u == 11:
                        merge_root(c - 1, fast)

            attention(0, 0, False)
            attention(1, 1, True)
            with act.Fori(1, CHUNKS // 2) as k:
                for par in range(2):
                    attention(2 * k + par, par, True)
            def message_hi(m, c, u):
                split_hi(c, M_PASS + m, u, (CHUNKS + m) * UNITS + u - SPLIT + 1)

            for u in range(SPLIT - 1):
                message_hi(0, 0, u)
            merge_copy(CHUNKS - 1, fast, acc[1], row[1])
            message_hi(0, 0, SPLIT - 1)
            merge_root(CHUNKS - 1, fast)
            act.activation(w_hi[:, :, :], both_w12, ACT.Copy).then_inc(w_hi_set, 1)

            act.wait_ge(flag_set, 1)
            with act.If(act.value_load(flag[0:1, 0:1], min_val=0, max_val=P) != 0):
                with act.Fori(0, CHUNKS) as c:
                    with act.Fori(0, BLOCKS) as j:
                        for s in range(2):
                            act.wait_ge(g_arg, c * (2 * BLOCKS) + j * 2 + s + 1)
                            act.activation(g_e, g_t, ACT.Exp).then_inc(g_exp, 1)
                    merge_copy(c, slow, acc[0], row[0])
                    merge_root(c, slow)
                act.wait_ge(slow["done"], CHUNKS + 1)

            def y_copy(m, par, split):
                act.wait_ge(unit_used, (CHUNKS + m + 1) * UNITS)
                wait(act, z2_set, m)
                act.activation(in_hi[:, :] if split else y[:, :], acc[par], ACT.Copy).then_inc(y_set, 1)

            def bias1(m, mlp):
                act.wait_ge(z1_set, m + 1)
                wait(act, fresh, m)
                act.activation(h1[:, :], z1, ACT.Identity, bias=mlp.b1).then_inc(bias1_set, 1)

            def h1_hi(m):
                act.wait_ge(h1_set, m + 1)
                act.activation(in_hi[:, :], h1[:, :], ACT.Copy).then_inc(h1_hi_set, 1)

            def bias2(m, mlp):
                act.wait_ge(z2_set, m + 1)
                wait(act, z3_set, m)
                act.activation(h2[:, :], z2, ACT.Identity, bias=mlp.b2).then_inc(bias2_set, 1)

            def fill_hi(r, s):
                if isinstance(r, int) and r == 0:
                    act.wait_ge(fast["done"], s + 1)
                else:
                    act.wait_ge(unit_used, ((r + 1) * CHUNKS - 1) * UNITS + (s + 1) * PER // UB)
                    act.wait_ge(fresh, (r - 1) * CHUNKS + s + 1)
                act.activation(u_hi[:, s * COLS:(s + 1) * COLS], stage[:, s * COLS:(s + 1) * COLS],
                               ACT.Relu if isinstance(r, int) and r == 0 else ACT.Copy).then_inc(u_hi_set, 1)

            def passing(r, c, par, mlp, prev, fills):
                m = r * CHUNKS + c
                begins = isinstance(r, int) and r == 0 and isinstance(c, int) and c == 0
                at = AT if is_split(c) else AT_UNSPLIT
                for u in range(UNITS):
                    if begins and u in fills:
                        fill_hi(*fills[u])
                    if not begins or u >= SPLIT:
                        message_hi(m, c, u)
                    if prev and u == at["y_copy"]:
                        y_copy(m - 1, 1 - par, is_split(c))
                    if prev and u == at["bias1"]:
                        bias1(m - 1, mlp)
                    if prev and u == at.get("h1_hi"):
                        h1_hi(m - 1)
                    if prev and u == at["bias2"]:
                        bias2(m - 1, mlp)
                    if not begins and u in fills:
                        fill_hi(*fills[u])

            def a_round(r, mlp, prev_mlp):
                passing(r, 0, 0, prev_mlp, prev_mlp is not None, fills_of(r))
                passing(r, 1, 1, mlp, True, {})
                with act.Fori(1, CHUNKS // 2 - 1) as k:
                    for par in range(2):
                        passing(r, 2 * k + par, par, mlp, True, {})
                passing(r, CHUNKS - 2, 0, mlp, True, {})
                passing(r, CHUNKS - 1, 1, mlp, True, fills_ahead(r + 1))

            a_round(0, uv, None)
            with act.Fori(0, (ROUNDS - 1) // 2) as q:
                a_round(2 * q + 1, vu, uv)
                a_round(2 * q + 2, uv, vu)
            m = ROUNDS * CHUNKS - 1
            act.wait_ge(unit_used, (CHUNKS + m + 1) * UNITS)
            act.wait_ge(z2_set, m)
            for cols in half_cols:
                act.activation(y[:, cols], acc[1][:, cols], ACT.Copy).then_inc(y_set, 1)
            act.wait_ge(fresh, m)
            for h, cols in enumerate(half_cols):
                act.wait_ge(z1_set, m + h + 1)
                act.activation(h1[:, cols], end_z1[h], ACT.Identity, bias=uv.b1).then_inc(bias1_set, 1)
            act.wait_ge(z3_set, m)
            for h, cols in enumerate(half_cols):
                act.wait_ge(z2_set, m + h + 1)
                act.activation(h2[:, cols], end_z2[h], ACT.Identity, bias=uv.b2).then_inc(bias2_set, 1)

        @block.vector
        def _(dve):
            def root(tile, links, s, n):
                dve.wait_ge(s["std"], n + 1)
                links(dve.reciprocal(tile[:, 2, :], tile[:, 1, :]))
                links(dve.tensor_tensor(tile[:, 3, :], tile[:, 2, :], tile[:, 2, :], ALU.mult))
                links(dve.tensor_tensor(tile[:, 4, :], tile[:, 3, :], tile[:, 0, :], ALU.mult))
                links(dve.tensor_scalar(tile[:, 5, :], tile[:, 4, :], -0.5, 1.5, ALU.mult, ALU.add))
                links(dve.tensor_tensor(tile[:, 6, :], tile[:, 5, :], tile[:, 2, :], ALU.mult))

            def split_lo(c, u, number):
                dve.wait_ge(hi_set, number)
                dve.tensor_tensor(a_lo[:, u % SPLIT, :], unit_raw(c, u), a_hi[:, u % SPLIT, :].bitcast(F32),
                                  ALU.subtract).then_inc(lo_set, 1)

            def pos_mask(c, u):
                dve.tensor_scalar(pos[u % SPLIT], unit_raw(c, u), 0.0, None, ALU.is_gt).then_inc(pos_by_dve, 1)

            def message_lo(m, c, u):
                split_lo(c, u, CHUNKS * SPLITS + m * UNITS + u + 1)

            def blk(t, n, b):
                at = n * COLS + b * P
                return t[:, at:at + P] if isinstance(n, int) else t[:, bass.ds(at, P)]

            def mask(c, u):
                wait_raw(dve, c, u)
                wait(dve, mask_used, c * UNITS + u - SPLIT + 1)
                dve.tensor_scalar(masks[:, u % SPLIT, 0, :], unit_raw(c, u), 0.0, None, ALU.is_gt)
                dve.tensor_scalar(masks[:, u % SPLIT, 1, :], unit_raw(c, u), 0.0, None, ALU.is_lt) \
                    .then_inc(masked, 1)

            link = Link(chain)
            for b in range(BLOCKS):
                if b % (BLOCKS // 4) == 0:
                    dve.wait_ge(x_in_sb[b // (BLOCKS // 4)], 16)
                ins = dve.bn_stats(stats0[:, b, :], x_sb[:, b * P:(b + 1) * P])
            link(ins)
            for b in range(BLOCKS):
                ins = dve.bn_aggr(mv0[:, b, :], stats0[:, b, :])
            link(ins)
            dve.tensor_scalar(root0[:, 0, :], mv0[:, :, 1], EPS, None, ALU.add).then_inc(first["var"], 1)
            root(root0, link, first, 0)

            def normalise(c, par):
                wait(dve, pre_t, c - 1)
                for b in range(PER):
                    j = c * PER + b
                    at = bass.ds(j, 1) if not isinstance(c, int) else slice(j, j + 1)
                    ins = dve.tensor_scalar(norm2[par][:, b * P:(b + 1) * P], blk(x_sb, c, b), mv0[:, at, 0],
                                            root0[:, 6, at], ALU.subtract, ALU.mult)
                ins.then_inc(first["done"], 1)

            def keep_p(c, par):
                dve.wait_ge(pre_hw, c + 1)
                cols = bass.ds(c * PER, PER) if not isinstance(c, int) else slice(c * PER, (c + 1) * PER)
                dve.wait_ge(pre_st, c + 1)
                dve.tensor_copy(p_all[:, cols, :].rearrange("p (k b) f -> p k b f", k=2),
                                hwp2[par][:, :, :, P:P + 2]).then_inc(pre_pc, 1)

            normalise(0, 0)
            normalise(1, 1)
            with dve.Fori(1, CHUNKS // 2) as k:
                for par in range(2):
                    normalise(2 * k + par, par)
                    keep_p(2 * k + par - 2, par)
            dve.wait_ge(kept_in, 16 * CHUNKS * KEPT)
            for u in range(SPLIT):
                mask(0, u)
            keep_p(CHUNKS - 2, 0)
            keep_p(CHUNKS - 1, 1)

            dve.wait_ge(pre_pc, CHUNKS)
            dve.memset(wpart[:, :, :], 0.0)
            link(dve.memset(probe[:, :, :], 0.0))
            dve.memset(probe[:, :, 13], 1.0)
            source = p_all
            for part in range(3):
                for k in range(2):
                    ins = dve.tensor_copy(probe[:, :, 3 * k + part], source[:, :, k])
                link(ins)
                for k in range(2):
                    ins = dve.tensor_copy(probe[:, :, 10 - 3 * k + part], source[:, :, k])
                    if part < 2:
                        ins = dve.tensor_tensor(rest[:, :, k], source[:, :, k], probe[:, :, 3 * k + part],
                                                ALU.subtract)
                if part < 2:
                    link(ins)
                source = rest
            ins.then_inc(probe_set, 1)

            def e_cols(c):
                dve.wait_ge(e_turned, c + 1)
                cols = bass.ds(c * PER, PER) if not isinstance(c, int) else slice(c * PER, (c + 1) * PER)
                dve.tensor_copy(e_all[:, cols, :],
                                tiny[:, 0:8 * PER].rearrange("p (b k) -> p b k", k=8)[:, :, 0:7]) \
                    .then_inc(e_col, 1)

            def mask_chunk(c, prev):
                for u in range(UNITS):
                    if prev or u >= SPLIT:
                        mask(c, u)
                    if prev and u == 6:
                        e_cols(c - 1)

            mask_chunk(0, False)
            with dve.Fori(1, CHUNKS) as c:
                mask_chunk(c, True)
            for u in range(KEPT):
                if u not in act_masks:
                    pos_mask(0, u)
                split_lo(0, u, u + 1)
            e_cols(CHUNKS - 1)

            dve.wait_ge(e_col, CHUNKS)
            for k in range(2):
                ins = dve.tensor_reduce(e_sum[:, :, k], e_all[:, :, 3 * k:3 * k + 3], AX.X, ALU.add)
            link(ins)
            link(dve.scalar_tensor_tensor(out=e_pm[:, :, :], in0=e_sum[:, :, :], scalar=E_SLOPE, in1=e_sum[:, :, :],
                                          op0=ALU.mult, op1=ALU.max))
            dve.tensor_reduce(top[:, 0:1], e_plus, AX.X, ALU.max).then_inc(top_part, 1)
            dve.tensor_scalar(noneg[:, :], e_all[:, :, 6], 0.5, None, ALU.is_lt)
            dve.wait_ge(top_all, 1)
            dve.tensor_scalar(e_sum[:, :, 0], e_plus, top[:, 1:2], TOP, ALU.subtract, ALU.add) \
                .then_inc(shifted, 1)
            dve.wait_ge(mask_used, CHUNKS * UNITS)

            def weight_lo(b):
                if b not in lo_fills:
                    return
                cols = slice(b * P, (b + 1) * P)
                dve.wait_ge(u_hi_set, fills.index(b) + 1)
                dve.scalar_tensor_tensor(out=u_lo[:, cols], in0=stage[:, cols], scalar=w_all[:, b:b + 1],
                                         in1=u_hi[:, cols].bitcast(F32), op0=ALU.mult, op1=ALU.subtract) \
                    .then_inc(u_lo_set, 1)

            def four(t, n):
                return t[:, n * PER:(n + 1) * PER] if isinstance(n, int) else t[:, bass.ds(n * PER, PER)]

            def merge(n, s):
                link = Link(s["chain"], n * MERGE_LINKS)
                dve.wait_ge(s["turned"], n + 1 + s["primed"])
                sums = tiny.rearrange("p (b g k) -> p b g k", b=PER, g=4)[:, :, :, 0:3]
                link(dve.tensor_reduce(four(den_all, n), sums, AX.XY, ALU.add))
                dve.scalar_tensor_tensor(out=four(ok_all, n), in0=four(den_all, n), scalar=LEAST,
                                         in1=four(noneg, n), op0=ALU.is_ge, op1=ALU.mult)
                link(dve.tensor_scalar(small[:, 7, :], four(den_all, n), TINY, None, ALU.max))
                link(dve.reciprocal(small[:, 7, :], small[:, 7, :]))
                link(dve.tensor_tensor(small[:, 7, :], small[:, 7, :], four(ok_all, n), ALU.mult))
                for b in range(PER):
                    old = blk(x_sb, n, b) if s is fast else blk(stage, n, b)
                    ins = dve.scalar_tensor_tensor(out=blk(x_sb, n, b), in0=tp[:, b * P:(b + 1) * P],
                                                   scalar=small[:, 7, b:b + 1], in1=old,
                                                   op0=ALU.mult, op1=ALU.add)
                link(ins, True)
                return link

            def merge_stats(n, s, link):
                for b in range(PER):
                    ins = dve.bn_stats(stats[:, b, :], blk(x_sb, n, b))
                link(ins, True)
                for b in range(PER):
                    ins = dve.bn_aggr(mv[:, b, :], stats[:, b, :])
                link(ins)
                dve.tensor_scalar(four(var_all, n), mv[:, :, 1], EPS, None, ALU.add)
                dve.tensor_scalar(small[:, 0, :], mv[:, :, 1], EPS, None, ALU.add).then_inc(s["var"], 1)
                assert link.k == 7

            def renorm(n, s, link):
                root(small, link, s, n)
                for b in range(PER):
                    ins = dve.tensor_scalar(blk(stage, n, b), blk(x_sb, n, b), mv[:, b, 0:1],
                                            small[:, 6, b:b + 1], ALU.subtract, ALU.mult)
                ins.then_inc(s["done"], 1)
                assert link.k == MERGE_LINKS

            def attention(c, prev):
                for u in range(UNITS):
                    if not prev:
                        if u:
                            for b in fills_at(u):
                                weight_lo(b)
                        if u == 2:
                            dve.wait_ge(hw_end_done, 16)
                            dve.wait_ge(u_lo_set, 1 + max(lo_fills.index(b) for b in range(28, 32)))
                    if u not in act_masks and (prev or u >= KEPT):
                        wait_raw(dve, A_PASS + c, u)
                        wait(dve, unit_used, c * UNITS + u - SPLIT + 2)
                        pos_mask(c, u)
                    if u not in DIRECT and (prev or u >= KEPT):
                        split_lo(c, u, c * SPLITS + split_no(u) + 1)
                    if prev and u == 8:
                        link = merge(c - 1, fast)
                    if prev and u == 9:
                        merge_stats(c - 1, fast, link)
                    if prev and u == 11:
                        renorm(c - 1, fast, link)

            for b in fills_at(0):
                weight_lo(b)
            dve.wait_ge(w_exp, 1)
            source = w_all
            for part in range(3):
                ins = dve.tensor_copy(wpart[:, :, part], source[:, :])
                if part < 2:
                    link(ins)
                    link(dve.tensor_tensor(rest[:, :, 0], source[:, :], wpart[:, :, part], ALU.subtract))
                    source = rest[:, :, 0]
            ins.then_inc(w_set, 1)
            early_links = link.k
            dve.wait_ge(w_set, 1)
            attention(0, False)
            dve.wait_ge(hw_done, 16)
            with dve.Fori(1, CHUNKS) as c:
                attention(c, True)
            for u in range(AHEAD_LO):
                message_lo(0, 0, u)
            last = merge(CHUNKS - 1, fast)
            merge_stats(CHUNKS - 1, fast, last)
            dve.wait_ge(fast["var"], CHUNKS)
            link = Link(chain, early_links)
            link(dve.scalar_tensor_tensor(out=w_all[:, :], in0=var_all[:, :], scalar=HUGE, in1=ok_all[:, :],
                                          op0=ALU.is_le, op1=ALU.mult))
            dve.tensor_reduce(good[:, :], w_all[:, :], AX.X, ALU.min).then_inc(good_set, 1)
            dve.wait_ge(good_sum, 1)
            dve.tensor_scalar(flag[:, :], tiny[:, 0:1], -1.0, float(P), ALU.mult, ALU.add).then_inc(flag_set, 1)
            renorm(CHUNKS - 1, fast, last)

            dve.wait_ge(flag_set, 1)
            with dve.If(dve.value_load(flag[0:1, 0:1], min_val=0, max_val=P) != 0):
                def maxima(c, u, b):
                    m = 2 * c * BLOCKS + u * UB + b
                    j = u * UB + b
                    glink = Link(g_chain, c * G_LINKS + 1 + (u * UB + b) * 5)
                    a = g_a[b]
                    dve.wait_ge(g_landed[b], c * (2 * UNITS * 16) + u * 16 + 16)
                    for k, there, absent in ((0, ALU.is_gt, ALU.is_le), (1, ALU.is_lt, ALU.is_ge)):
                        dve.tensor_scalar(g_t, a, 0.0, e_pm[:, bass.ds(j, 1), k], there, ALU.mult)
                        glink(dve.tensor_scalar(g_s, a, 0.0, -HUGE, absent, ALU.mult))
                        glink(dve.tensor_tensor(g_t, g_t, g_s, ALU.add))
                        ins = dve.tensor_tensor(g_row, g_row, g_t, ALU.max)
                        if k == 0:
                            glink(ins)
                    ins.then_inc(g_freed, 1)
                    dve.wait_ge(g_freed, m + 2)

                def weights(c, u, b):
                    m = (2 * c + 1) * BLOCKS + u * UB + b
                    n = c * BLOCKS + u * UB + b
                    j = u * UB + b
                    glink = Link(g_chain, c * G_LINKS + 2 + BLOCKS * 5 + (u * UB + b) * 3)
                    a = g_a[b]
                    dve.wait_ge(g_landed[b], c * (2 * UNITS * 16) + (UNITS + 1) * 16 + u * 16)
                    dve.tensor_scalar(g_t, g_neg, e_pm[:, bass.ds(j, 1), 0], 0.0, ALU.add, ALU.min).then_inc(g_arg, 1)
                    dve.wait_ge(g_prod, n + 1)
                    dve.wait_ge(g_exp, 2 * n + 1)
                    dve.scalar_tensor_tensor(out=g_num, in0=a, scalar=0.0, in1=g_e, op0=ALU.max, op1=ALU.mult)
                    glink(dve.scalar_tensor_tensor(out=g_den, in0=a, scalar=0.0, in1=g_e,
                                                   op0=ALU.is_gt, op1=ALU.mult))
                    dve.tensor_scalar(g_t, g_neg, e_pm[:, bass.ds(j, 1), 1], 0.0, ALU.add, ALU.min).then_inc(g_arg, 1)
                    dve.wait_ge(g_exp, 2 * n + 2)
                    glink(dve.scalar_tensor_tensor(out=g_s, in0=a, scalar=0.0, in1=g_e, op0=ALU.min, op1=ALU.mult))
                    glink(dve.tensor_tensor(g_num, g_num, g_s, ALU.add))
                    dve.scalar_tensor_tensor(out=g_s, in0=a, scalar=0.0, in1=g_e,
                                             op0=ALU.is_lt, op1=ALU.mult).then_inc(g_freed, 1)
                    dve.wait_ge(g_freed, m + 2)
                    dve.tensor_tensor(g_den, g_den, g_s, ALU.add).then_inc(g_tile, 1)

                for k, s in enumerate((g_freed, g_prod, slow["turned"], slow["done"])):
                    dve.memset(gate[:, k + 2:k + 3], 0.0).then_inc(s, 1)
                dve.memset(noneg[:, :], 1.0).then_inc(g_noneg, 1)
                dve.wait_ge(g_noneg, 1)
                dve.wait_ge(g_x, 16)
                with dve.Fori(0, CHUNKS) as c:
                    glink = Link(g_chain, c * G_LINKS)
                    glink(dve.memset(g_row, -HUGE), True)
                    with dve.Fori(0, UNITS) as u:
                        for b in range(UB):
                            maxima(c, u, b)
                    dve.wait_ge(g_all, c + 1)
                    dve.tensor_scalar(g_neg, g_e, -1.0, None, ALU.mult).then_inc(g_chain, 1)
                    dve.wait_ge(g_chain, c * G_LINKS + 2 + BLOCKS * 5)
                    dve.memset(gate[:, 0:1], 0.0)
                    with dve.Fori(0, UNITS) as u:
                        for b in range(UB):
                            weights(c, u, b)
                    own = merge(c, slow)
                    merge_stats(c, slow, own)
                    renorm(c, slow, own)
                    dve.wait_ge(slow["done"], c + 2)

            def fill_lo(s, op):
                cols = slice(s * COLS, (s + 1) * COLS)
                dve.scalar_tensor_tensor(out=u_lo[:, cols], in0=stage[:, cols], scalar=0.0 if op is ALU.max else 1.0,
                                         in1=u_hi[:, cols].bitcast(F32), op0=op, op1=ALU.subtract) \
                    .then_inc(u_lo_set, 1)

            def leaky(h, ready, m, done, cols=slice(0, COLS)):
                dve.wait_ge(ready, m + 1)
                dve.scalar_tensor_tensor(out=h[:, cols], in0=h[:, cols], scalar=SLOPE, in1=h[:, cols],
                                         op0=ALU.mult, op1=ALU.max).then_inc(done, 1)

            def rest_of(t, done):
                dve.tensor_tensor(in_lo[:, :], t, in_hi[:, :].bitcast(F32), ALU.subtract).then_inc(done, 1)

            def features(m, c, mlp):
                dve.wait_ge(z3_set, m + 1)
                dve.tensor_tensor(h1[:, :].rearrange("p (b f) -> p b f", b=PER),
                                  tp.rearrange("p (b f) -> p b f", b=PER), mlp.b3, ALU.add).then_inc(t3_set, 1)
                dve.wait_ge(t3_set, m + 1)
                dve.scalar_tensor_tensor(out=stage[:, chunk_cols(c)], in0=h1[:, :], scalar=SLOPE, in1=h1[:, :],
                                         op0=ALU.mult, op1=ALU.max).then_inc(fresh, 1)

            def passing(r, c, par, mlp, prev, prev_c, fills):
                m = r * CHUNKS + c

                def fill():
                    of, s = fills[u]
                    dve.wait_ge(u_hi_set, BLOCKS + of * CHUNKS + s + 1)
                    fill_lo(s, ALU.max if isinstance(of, int) and of == 0 else ALU.mult)

                begins = isinstance(r, int) and r == 0 and isinstance(c, int) and c == 0
                at = AT if is_split(c) else AT_UNSPLIT
                for u in range(UNITS):
                    if begins and u in fills:
                        fill()
                    if begins and u == AHEAD_LO - 1:
                        dve.wait_ge(w_hi_set, 1)
                        dve.tensor_tensor(w_lo[:, :, :], both_w12, w_hi[:, :, :].bitcast(F32), ALU.subtract) \
                            .then_inc(w_lo_set, 1)
                    if not begins or u >= AHEAD_LO:
                        message_lo(m, c, u)
                    if prev and u == at.get("y_lo"):
                        dve.wait_ge(y_set, m)
                        rest_of(acc[1 - par], y_lo_set)
                    if prev and u == at["leaky1"]:
                        leaky(h1, bias1_set, m - 1, h1_set)
                    if prev and u == at.get("h1_lo"):
                        dve.wait_ge(h1_hi_set, split_mlp_no(r, c))
                        rest_of(h1[:, :], h1_lo_set)
                    if prev and u == at["leaky2"]:
                        leaky(h2, bias2_set, m - 1, h2_set)
                    if prev and u == at["features"]:
                        features(m - 1, prev_c, mlp)
                    if not begins and u in fills:
                        fill()

            def a_round(r, mlp, prev_mlp):
                passing(r, 0, 0, prev_mlp, prev_mlp is not None, CHUNKS - 1, fills_of(r))
                with dve.Fori(0, CHUNKS // 2 - 1) as k:
                    for par in (1, 0):
                        c = 2 * k + 2 - par
                        passing(r, c, par, mlp, True, c - 1, {})
                passing(r, CHUNKS - 1, 1, mlp, True, CHUNKS - 2, fills_ahead(r + 1))

            a_round(0, uv, None)
            with dve.Fori(0, (ROUNDS - 1) // 2) as q:
                a_round(2 * q + 1, vu, uv)
                a_round(2 * q + 2, uv, vu)
            m = ROUNDS * CHUNKS - 1

            def result(c):
                cols = slice(c * COLS, (c + 1) * COLS)
                dve.wait_ge(fresh, (ROUNDS - 1) * CHUNKS + c + 1)
                dve.tensor_tensor(stage[:, cols], stage[:, cols], x_sb[:, cols], ALU.add).then_inc(final, 1)

            for c in range(CHUNKS - 1):
                result(c)
            for h, cols in enumerate(half_cols):
                leaky(h1, bias1_set, m + h, h1_set, cols)
            for h, cols in enumerate(half_cols):
                leaky(h2, bias2_set, m + h, h2_set, cols)
            blocks = PER // HALVES
            for h, cols in enumerate(half_cols):
                at = slice(N - COLS + cols.start, N - COLS + cols.stop)
                dve.wait_ge(z3_set, m + h + 1)
                dve.tensor_tensor(h1[:, cols].rearrange("p (b f) -> p b f", b=blocks),
                                  end_z3[h].rearrange("p (b f) -> p b f", b=blocks), uv.b3[:, 0:blocks, :],
                                  ALU.add).then_inc(t3_set, 1)
                dve.wait_ge(t3_set, m + h + 1)
                dve.scalar_tensor_tensor(out=stage[:, at], in0=h1[:, cols], scalar=SLOPE, in1=h1[:, cols],
                                         op0=ALU.mult, op1=ALU.max).then_inc(fresh, 1)
                dve.wait_ge(fresh, m + h + 1)
                dve.tensor_tensor(stage[:, at], stage[:, at], x_sb[:, at], ALU.add).then_inc(final, 1)

        @block.tensor
        def _(pe):
            pe.wait_ge(params_in_sb, 16)
            pe.wait_ge(pick_set, 1)
            w0 = params[:, W0:W0 + P]
            pe.transpose(acc[0][:, 0:P], w0, ident).then_inc(w0_turned, 1)
            pe.wait_ge(w0_copied, 1)
            pe.matmul(acc[1][:, 0:2], stage[:, 0:P], a12, start=True, stop=True).then_inc(w0a_summed, 1)
            pe.wait_ge(w0a_set, 1)

            def turn_in(c, par):
                pe.wait_ge(first["done"], c + 1)
                wait(pe, pre_y, c - 1)
                for b in range(PER):
                    cols = slice(b * P, (b + 1) * P)
                    mm = pe.transpose(turned2[par][:, cols], norm2[par][:, cols], ident)
                mm.then_inc(pre_t, 1)

            def project(c, par):
                pe.wait_ge(pre_y, c + 1)
                wait(pe, pre_pc, c - 1)
                for b in range(PER):
                    mm = pe.matmul(hwp2[par][:, b // 2, b % 2, :], hwt2[par][:, b * P:(b + 1) * P],
                                   params[:, W0:W0 + P + 2], start=True, stop=True)
                mm.then_inc(pre_hw, 1)

            turn_in(0, 0)
            turn_in(1, 1)
            project(0, 0)
            turn_in(2, 0)
            project(1, 1)
            with pe.Fori(1, CHUNKS // 2 - 1) as k:
                for par in range(2):
                    turn_in(2 * k + par + 1, 1 - par)
                    project(2 * k + par, par)
            turn_in(CHUNKS - 1, 1)
            project(CHUNKS - 2, 0)
            project(CHUNKS - 1, 1)

            def e_turn(c):
                pe.wait_ge(params_in_sb, 16)
                pe.wait_ge(e_row, c + 1)
                wait(pe, e_col, c)
                for b in range(PER):
                    mm = pe.transpose(tiny[:, 8 * b:8 * b + 7], y[0:7, b * P:(b + 1) * P], ident[0:7, 0:7])
                mm.then_inc(e_turned, 1)

            def e_chunk(c, par, prev):
                wait(pe, e_row, c - 1)
                for u in range(UNITS):
                    pe.wait_ge(masked, c * UNITS + u + 1)
                    for b in range(UB):
                        j = u * UB + b
                        for g in range(2):
                            mm = pe.matmul(row[par][0:7, :], probe[:, j, 7 * g:7 * g + 7],
                                           masks[:, u % SPLIT, g, b * COLS:(b + 1) * COLS],
                                           start=(j == 0 and g == 0), stop=(j == BLOCKS - 1 and g == 1))
                    mm.then_inc(mask_used, 1)
                    if prev and u == 3:
                        e_turn(c - 1)

            pe.wait_ge(probe_set, 1)
            for par in range(2):
                e_chunk(par, par, par == 1)
            with pe.Fori(1, CHUNKS // 2) as k:
                for par in range(2):
                    e_chunk(2 * k + par, par, True)
            e_turn(CHUNKS - 1)

            def split_products(par, u, number, stationary_ready):
                pe.wait_ge(hi_set, number)
                pe.wait_ge(lo_set, number)
                for b in range(UB):
                    j = u * UB + b
                    stationary_ready(j)
                    cols, mov = slice(j * P, (j + 1) * P), slice(b * COLS, (b + 1) * COLS)
                    hi, lo = a_hi[:, u % SPLIT, mov], a_lo[:, u % SPLIT, mov]
                    pe.matmul(acc[par], u_hi[:, cols], hi, start=(j == 0), stop=False)
                    pe.matmul(acc[par], u_hi[:, cols], lo, start=False, stop=False)
                    mm = pe.matmul(acc[par], u_lo[:, cols], hi, start=False, stop=(j == BLOCKS - 1))
                mm.then_inc(unit_used, 1)

            def attention_products(m_abs, par, u):
                if u % 2:
                    pe.wait_ge(pos_by_dve, masks_made(False, m_abs, u))
                    pe.wait_ge(pos_by_act, masks_made(True, m_abs, u))
                    if isinstance(m_abs, int) and m_abs == 0 and u == 1:
                        pe.wait_ge(w_set, 1)
                    for g in range(2 * UB):
                        j = (u - 1) * UB + g
                        pe.matmul(psum[32 * g:32 * g + 32, 2 + par, :], wpart[:, j, :],
                                  pos[(j // UB) % SPLIT][:, (j % UB) * COLS:(j % UB + 1) * COLS],
                                  start=(u == 1), stop=(u == UNITS - 1), tile_position=(0, 32 * g))

                first = isinstance(m_abs, int) and m_abs == 0
                if u not in DIRECT:
                    def ready(j):
                        if first:
                            pe.wait_ge(u_lo_set, lo_fills.index(j) + 1)
                    split_products(par, u, m_abs * SPLITS + split_no(u) + 1, ready)
                    return
                wait_raw(pe, A_PASS + m_abs, u)
                for b in range(UB):
                    j = u * UB + b
                    if first:
                        pe.wait_ge(u_hi_set, fills.index(j) + 1)
                    mm = pe.matmul(acc[par], scratch[:, j * P:(j + 1) * P],
                                   unit_raw(m_abs, u)[:, b * COLS:(b + 1) * COLS], start=False, stop=False)
                mm.then_inc(unit_used, 1)

            def turn(n, s):
                pe.wait_ge(s["copied"], n + 1)
                wait(pe, s["done"], n + s["primed"])
                for b in range(PER):
                    pe.transpose(tp[:, b * P:(b + 1) * P], y[:, b * P:(b + 1) * P], ident)
                for b in range(PER):
                    mm = pe.transpose(tiny[:, b * P:(b + 1) * P], h2[:, b * P:(b + 1) * P], ident)
                mm.then_inc(s["turned"], 1)

            def attention(c, par, prev):
                wait(pe, fast["copied"], c - 1)
                for u in range(UNITS):
                    attention_products(c, par, u)
                    if prev and u == 5:
                        turn(c - 1, fast)

            attention(0, 0, False)
            attention(1, 1, True)
            with pe.Fori(1, CHUNKS // 2) as k:
                for par in range(2):
                    attention(2 * k + par, par, True)
            turn(CHUNKS - 1, fast)

            pe.wait_ge(good_set, 1)
            pe.matmul(tiny[:, 0:1], pick[:, :], good[:, :], start=True, stop=True).then_inc(good_sum, 1)
            pe.wait_ge(flag_set, 1)
            with pe.If(pe.value_load(flag[0:1, 0:1], min_val=0, max_val=P) != 0):
                def tile(c, u, b, begin, end):
                    n = c * BLOCKS + u * UB + b
                    pe.wait_ge(hw_landed[b], c * (UNITS * 16) + u * 16 + 16)
                    pe.wait_ge(g_tile, n + 1)
                    pe.matmul(acc[0], g_hw[b], g_num, start=begin, stop=end)
                    pe.matmul(row[0], pick[:, :], g_den, start=begin, stop=end).then_inc(g_prod, 1)

                with pe.Fori(0, CHUNKS) as c:
                    tile(c, 0, 0, True, False)
                    tile(c, 0, 1, False, False)
                    with pe.Fori(1, UNITS - 1) as u:
                        tile(c, u, 0, False, False)
                        tile(c, u, 1, False, False)
                    tile(c, UNITS - 1, 0, False, False)
                    tile(c, UNITS - 1, 1, False, True)
                    turn(c, slow)

            def layer(z, w, k, t, split):
                if split is None:
                    return pe.matmul(z, w.w[k], t[:, :], start=True, stop=True)
                pe.matmul(z, w.hi[k], in_hi[:, :], start=True, stop=False)
                pe.matmul(z, w.hi[k], in_lo[:, :], start=False, stop=False)
                return pe.matmul(z, w.lo[k], in_hi[:, :], start=False, stop=True)

            def mlp1(m, mlp, split):
                pe.wait_ge(y_set, m + 1) if split is None else pe.wait_ge(y_lo_set, split)
                wait(pe, bias1_set, m)
                layer(z1, mlp, 0, y, split).then_inc(z1_set, 1)

            def mlp2(m, mlp, split):
                pe.wait_ge(h1_set, m + 1) if split is None else pe.wait_ge(h1_lo_set, split)
                wait(pe, bias2_set, m)
                layer(z2, mlp, 1, h1, split).then_inc(z2_set, 1)

            def mlp3(m, mlp):
                pe.wait_ge(h2_set, m + 1)
                wait(pe, t3_set, m)
                for b in range(PER):
                    mm = pe.matmul(tp[:, b * P:(b + 1) * P], h2[:, b * P:(b + 1) * P], mlp.w[2],
                                   start=True, stop=True)
                mm.then_inc(z3_set, 1)

            def passing(r, c, par, mlp, prev, start):
                m = r * CHUNKS + c
                if isinstance(m, int) and m == 1:
                    pe.wait_ge(w_lo_set, 1)
                if is_split(c) and not (isinstance(c, int) and c == 1) or c == CHUNKS - 1:
                    pe.wait_ge(y_lo_set, split_mlp_no(r, c - 1))
                else:
                    wait(pe, y_set, m - 1)
                split = split_mlp_no(r, c) if is_split(c) else None
                at = AT if is_split(c) else AT_UNSPLIT
                for u in range(UNITS):
                    def ready(j):
                        if start and j % PER == 0:
                            pe.wait_ge(u_lo_set, LO_FILLS + r * CHUNKS + j // PER + 1)
                    split_products(par, u, CHUNKS * SPLITS + m * UNITS + u + 1, ready)
                    if prev and u == at["mlp1"]:
                        mlp1(m - 1, mlp, split)
                    if prev and u == at["mlp2"]:
                        mlp2(m - 1, mlp, split)
                    if prev and u == at["mlp3"]:
                        mlp3(m - 1, mlp)

            def a_round(r, mlp, prev_mlp):
                passing(r, 0, 0, prev_mlp, prev_mlp is not None, True)
                passing(r, 1, 1, mlp, True, False)
                with pe.Fori(1, CHUNKS // 2 - 1) as k:
                    for par in range(2):
                        passing(r, 2 * k + par, par, mlp, True, False)
                passing(r, CHUNKS - 2, 0, mlp, True, False)
                passing(r, CHUNKS - 1, 1, mlp, True, False)

            a_round(0, uv, None)
            with pe.Fori(0, (ROUNDS - 1) // 2) as q:
                a_round(2 * q + 1, vu, uv)
                a_round(2 * q + 2, uv, vu)
            m = ROUNDS * CHUNKS - 1
            for h, cols in enumerate(half_cols):
                pe.wait_ge(y_set, m + h + 1)
                pe.matmul(end_z1[h], uv.w[0], y[:, cols], start=True, stop=True).then_inc(z1_set, 1)
            for h, cols in enumerate(half_cols):
                pe.wait_ge(h1_set, m + h + 1)
                pe.matmul(end_z2[h], uv.w[1], h1[:, cols], start=True, stop=True).then_inc(z2_set, 1)
            for h, cols in enumerate(half_cols):
                pe.wait_ge(h2_set, m + h + 1)
                for b in range(PER // HALVES):
                    at = cols.start + b * P
                    mm = pe.matmul(end_z3[h][:, b * P:(b + 1) * P], h2[:, at:at + P], uv.w[2],
                                   start=True, stop=True)
                mm.then_inc(z3_set, 1)


def kernel(x, adj, L0_gnn_W, L0_gnn_a, L1_gnn_v_node_feats, L1_gnn_uv_W1, L1_gnn_uv_b1, L1_gnn_uv_W2,
           L1_gnn_uv_b2, L1_gnn_uv_W3, L1_gnn_uv_b3, L1_gnn_vu_W1, L1_gnn_vu_b1, L1_gnn_vu_W2,
           L1_gnn_vu_b2, L1_gnn_vu_W3, L1_gnn_vu_b3):
    import numpy as np
    import concourse.bacc as bacc
    from concourse.bass_utils import run_bass_kernel_spmd

    a = np.asarray(adj).reshape(P, CHUNKS, PER, P, UNITS, UB).transpose(1, 4, 3, 5, 2, 0)
    a = np.ascontiguousarray(a).reshape(CHUNKS * UNITS, P, UW)
    rows = [np.broadcast_to(np.asarray(b)[None, :], (P, P)) for b in (L1_gnn_uv_b3, L1_gnn_vu_b3)]
    columns = [np.asarray(b)[:, None] for b in (L1_gnn_uv_b1, L1_gnn_uv_b2, L1_gnn_vu_b1, L1_gnn_vu_b2)]
    halves = np.asarray(L0_gnn_a).reshape(2, P).transpose()
    params = np.concatenate(
        [np.asarray(w) for w in (L1_gnn_uv_W1, L1_gnn_uv_W2, L1_gnn_uv_W3, L1_gnn_vu_W1,
                                 L1_gnn_vu_W2, L1_gnn_vu_W3)]
        + rows + [np.eye(P, dtype=np.float32), halves] + columns
        + [np.asarray(L0_gnn_W)], axis=1)
    arrays = {"x_in": np.ascontiguousarray(np.asarray(x)).reshape(P, N), "adj_in": a,
              "params_in": np.ascontiguousarray(params)}

    nc = bacc.Bacc("TRN2", target_bir_lowering=False, num_devices=1)
    ins = {k: nc.dram_tensor(k, v.shape, F32, kind="ExternalInput").ap() for k, v in arrays.items()}
    out = nc.dram_tensor("out", (P, N), F32, kind="ExternalOutput").ap()
    hw_dram = nc.dram_tensor("hw_dram", (P, N), F32, kind="Internal").ap()
    build(nc, ins["x_in"], ins["adj_in"], ins["params_in"], out, hw_dram)
    got = run_bass_kernel_spmd(nc, [arrays], core_ids=[0])
    return np.asarray(got.results[0]["out"]).reshape(N, P)
```
